# Optimizing a Trainium2 kernel written in Bass

```python
import numpy as np
import jax
import jax.numpy as jnp

def _softmax(x, axis=-1):
    return jax.nn.softmax(x, axis=axis)

def _gelu(x):
    return jax.nn.gelu(x, approximate=True)

def _silu(x):
    return jax.nn.silu(x)

def _sigmoid(x):
    return jax.nn.sigmoid(x)

def _layernorm(x, axis=-1, eps=1e-05):
    m = jnp.mean(x, axis=axis, keepdims=True)
    v = jnp.var(x, axis=axis, keepdims=True)
    return (x - m) / jnp.sqrt(v + eps)

def _scatter_add(tgt, idx, src, axis=0):
    return tgt.at[idx].add(src)

def _segment_sum(src, seg, n):
    return jax.ops.segment_sum(src, seg, n)
kernel_name = 'mk_sandwich_d1_jaxref_r4_d85eda'

def setup_inputs(seed: int=0):
    np.random.seed(seed)
    _w = jnp.asarray

    def _L0_attn_setup():
        import jax, jax.numpy as jnp
        import numpy as np
        import math
        B, L, D, N2 = (8, 1024, 256, 32)

        def s4d_kernel(log_dt, log_A_real, A_imag, C_real, C_imag, length):
            dt = jnp.exp(log_dt)[:, None]
            A = -jnp.exp(log_A_real) + 1j * A_imag
            dtA = A * dt
            C = (C_real + 1j * C_imag) * (jnp.exp(dtA) - 1.0) / A
            t = jnp.arange(length, dtype=jnp.float32)
            vand = jnp.exp(dtA[:, :, None] * t)
            K = 2.0 * jnp.einsum('dn,dnl->dl', C, vand).real
            return K
        key = jax.random.key(seed)
        ks = jax.random.split(key, 6)
        x = jax.random.normal(ks[0], (B, L, D), dtype=jnp.float32)
        log_dt = jax.random.uniform(ks[1], (D,), minval=math.log(0.001), maxval=math.log(0.1)).astype(jnp.float32)
        log_A_real = jnp.log(0.5 * jnp.ones((D, N2), jnp.float32))
        A_imag = math.pi * jnp.broadcast_to(jnp.arange(N2, dtype=jnp.float32), (D, N2))
        C_real = jax.random.normal(ks[2], (D, N2), dtype=jnp.float32)
        C_imag = jax.random.normal(ks[3], (D, N2), dtype=jnp.float32)
        W = jax.random.normal(ks[4], (D, D), dtype=jnp.float32) / jnp.sqrt(jnp.float32(D))
        b = jax.random.normal(ks[5], (D,), dtype=jnp.float32) * 0.01
        return dict(x=x, log_dt=log_dt, log_A_real=log_A_real, A_imag=A_imag, C_real=C_real, C_imag=C_imag, W=W, b=b)
    _L0_attn_in = _L0_attn_setup()

    def _L0_ffn_setup():
        import jax, jax.numpy as jnp
        import numpy as np
        NUM_EXPERTS = 8
        D_MODEL = 256
        D_FF = 1024
        BATCH, SEQ = (2, 1024)
        key = jax.random.key(seed)
        k_x, k_w1, k_w2 = jax.random.split(key, 3)
        x = jax.random.normal(k_x, (BATCH, SEQ, D_MODEL), dtype=jnp.float32)
        w1 = jax.random.normal(k_w1, (NUM_EXPERTS, D_MODEL, D_FF), dtype=jnp.float32) * (1.0 / np.sqrt(D_MODEL))
        b1 = jnp.zeros((NUM_EXPERTS, D_FF), dtype=jnp.float32)
        w2 = jax.random.normal(k_w2, (NUM_EXPERTS, D_FF, D_MODEL), dtype=jnp.float32) * (1.0 / np.sqrt(D_FF))
        b2 = jnp.zeros((NUM_EXPERTS, D_MODEL), dtype=jnp.float32)
        return {'x': x, 'w1': w1, 'b1': b1, 'w2': w2, 'b2': b2}
    _L0_ffn_in = _L0_ffn_setup()
    _d = {'L0_attn_x': _L0_attn_in['x'], 'L0_attn_log_dt': _L0_attn_in['log_dt'], 'L0_attn_log_A_real': _L0_attn_in['log_A_real'], 'L0_attn_A_imag': _L0_attn_in['A_imag'], 'L0_attn_C_real': _L0_attn_in['C_real'], 'L0_attn_C_imag': _L0_attn_in['C_imag'], 'L0_attn_W': _L0_attn_in['W'], 'L0_attn_b': _L0_attn_in['b'], 'L0_ffn_w1': _L0_ffn_in['w1'], 'L0_ffn_b1': _L0_ffn_in['b1'], 'L0_ffn_w2': _L0_ffn_in['w2'], 'L0_ffn_b2': _L0_ffn_in['b2']}
    _x0 = _d['L0_attn_x']
    _d['L0_attn_x'] = jax.random.normal(jax.random.fold_in(jax.random.key(seed), 1), (8, 1024, 256), dtype=_x0.dtype)
    del _x0
    return _d

def reference(L0_attn_x, L0_attn_log_dt, L0_attn_log_A_real, L0_attn_A_imag, L0_attn_C_real, L0_attn_C_imag, L0_attn_W, L0_attn_b, L0_ffn_w1, L0_ffn_b1, L0_ffn_w2, L0_ffn_b2):

    def _L0_attn_ref(x, log_dt, log_A_real, A_imag, C_real, C_imag, W, b):
        import jax, jax.numpy as jnp
        import numpy as np
        import math
        B, L, D, N2 = (8, 1024, 256, 32)

        def s4d_kernel(log_dt, log_A_real, A_imag, C_real, C_imag, length):
            dt = jnp.exp(log_dt)[:, None]
            A = -jnp.exp(log_A_real) + 1j * A_imag
            dtA = A * dt
            C = (C_real + 1j * C_imag) * (jnp.exp(dtA) - 1.0) / A
            t = jnp.arange(length, dtype=jnp.float32)
            vand = jnp.exp(dtA[:, :, None] * t)
            K = 2.0 * jnp.einsum('dn,dnl->dl', C, vand).real
            return K
        Bb, Ll, Dd = x.shape
        K = s4d_kernel(log_dt, log_A_real, A_imag, C_real, C_imag, Ll)
        n_fft = 2 * Ll
        x_t = jnp.transpose(x, (0, 2, 1))
        k_f = jnp.fft.rfft(K, n=n_fft)
        x_f = jnp.fft.rfft(x_t, n=n_fft)
        y = jnp.fft.irfft(x_f * k_f[None], n=n_fft)[:, :, :Ll]
        y = jnp.transpose(y, (0, 2, 1))
        y = jax.nn.gelu(y, approximate=False)
        return y @ W.T + b

    def _L0_ffn_ref(x, w1, b1, w2, b2):
        import jax, jax.numpy as jnp
        import numpy as np
        NUM_EXPERTS = 8
        D_MODEL = 256
        D_FF = 1024
        BATCH, SEQ = (2, 1024)
        B, S, D = x.shape
        E = w1.shape[0]
        T = B * S // E
        tokens = x.reshape(E, T, D)
        h = jnp.einsum('etd,edf->etf', tokens, w1) + b1[:, None, :]
        h = jax.nn.gelu(h)
        y = jnp.einsum('etf,efd->etd', h, w2) + b2[:, None, :]
        return y.reshape(B, S, D)
    x = L0_attn_x
    x = x + _layernorm(_L0_attn_ref(_layernorm(x, axis=-1), L0_attn_log_dt, L0_attn_log_A_real, L0_attn_A_imag, L0_attn_C_real, L0_attn_C_imag, L0_attn_W, L0_attn_b), axis=-1)
    x = x + _layernorm(_L0_ffn_ref(_layernorm(x, axis=-1), L0_ffn_w1, L0_ffn_b1, L0_ffn_w2, L0_ffn_b2), axis=-1)
    return x

_drawn_inputs = setup_inputs


def setup_inputs(seed=0):
    import zlib

    import numpy as np

    out = dict(_drawn_inputs(seed))
    spreads = {'L0_attn_log_A_real': (-0.6931471824645996, 0.2),
     'L0_ffn_b1': (0.0, 0.1),
     'L0_ffn_b2': (0.0, 0.1)}
    factors = {'L0_attn_b': 5.985}
    for name, (base, spread) in spreads.items():
        noise = np.random.default_rng([zlib.crc32(name.encode()), seed]).standard_normal(out[name].shape)
        drawn = base * np.exp(spread * noise) if base else spread * noise
        out[name] = jnp.asarray(drawn.astype(out[name].dtype))
    for name, factor in factors.items():
        out[name] = (out[name] * factor).astype(out[name].dtype)
    return out
```

```python
from contextlib import ExitStack

import concourse.bass as bass
from concourse import mybir

F32 = mybir.dt.float32
F16 = mybir.dt.float16
I32 = mybir.dt.int32
ALU = mybir.AluOpType
ACT = mybir.ActivationFunctionType

P = 128
B, L, D = 8, 1024, 256
N = 32
E, F = 8, 1024
C = L // P
CB = C * B
SB = (C - 1) * B
J = P // N
Q = D // J
T = P + 1
GQ = 8
GC = GQ * J
G = Q // GQ
KD = D // P
KF = F // P
ST = 4
EPS = 1e-5
PI = 3.14159265358979
TWO_PI = 6.283185
INV_2PI = 0.15915494309189535
PI_HI, PI_LO = 6.28125, 0.0019353071795864769
LN2_HI, LN2_LO = 0.693359375, -2.12194440054690583e-4
EXP_STEPS = 15
MAGIC = 12582912.0
Y_SCALE, W_SCALE = 64.0, 64.0
C_ID, C_REV, C_POW, C_MASK = 0, P, 2 * P, 2 * P + T
C_END = C_MASK + GQ * GC


def mixer_prologue(nc, io, sh):
    with ExitStack() as ctx:
        def sb(name, shape, dt=F32):
            return ctx.enter_context(nc.sbuf_tensor(name, shape, dt))

        def sem(name):
            return ctx.enter_context(nc.semaphore(name))

        par = sb("par", [Q, 3, P])
        logs = sb("logs", [Q, P + J])
        ex = sb("ex", [Q, 5, P + J])
        w = sb("w", [Q, 24, P])
        res = sb("res", [Q, 6, P])
        xraw = sb("xraw", [P, 2, C, D])
        stats = sb("stats", [P, 2, C, 6])
        small = sb("small", [P, 2, 6, C])
        minus_half = sb("minus_half", [P, C])
        rstd = sb("rstd", [P, 2, C])
        earg = sb("earg", [P, 2, GQ, T])
        zeros = sb("zeros", [P, KD, P])
        ps = ctx.enter_context(nc.psum_tensor("psP", [P, 6, Q], F32))

        par_in, x_in, const_in = sem("par_in"), [sem("x_in0"), sem("x_in1")], sem("const_in")
        x_free, stat_step, var_ready, rstd_ready, xn_step = (
            sem("x_free"), sem("stat_step"), sem("var_ready"), sem("rstd_ready"), sem("xn_step"))
        par_step, act_par, turned, par_ready = sem("par_step"), sem("act_par"), sem("turned"), sem("par_ready")
        cst, earg_ready, e_done, pad_done = sem("cst"), sem("earg_ready"), sem("e_done"), sem("pad_done")

        ident = sh["const"][:, C_ID:C_ID + P]
        tcol = sh["const"][:, C_POW:C_POW + T]
        block = ctx.enter_context(nc.Block())

        @block.sync
        def _(sp):
            sp.dma_start(logs[:, 0:P], io["log_A_real"].rearrange("(q j) n -> q (j n)", j=J)).then_inc(par_in, 16)
            for k, name in enumerate(("A_imag", "C_real", "C_imag")):
                sp.dma_start(par[:, k, :], io[name].rearrange("(q j) n -> q (j n)", j=J)).then_inc(par_in, 16)
            sp.dma_start(logs[:, P:P + J], io["log_dt"].rearrange("(q j) -> q j", j=J)).then_inc(par_in, 16)
            sp.dma_start(sh["const"][:], io["const"]).then_inc(const_in, 16)
            for b in range(B):
                sp.wait_ge(x_free, b + 1)
                sp.dma_start(xraw[:, b % 2], io["x"][b].rearrange("(c p) d -> p c d", p=P)).then_inc(x_in[b % 2], 16)
            sp.wait_ge(cst, 1)
            sp.dma_start(io["kpad"].rearrange("(h p) t -> p h t", p=P)[:, :, P:2 * P], zeros[:]).then_inc(pad_done, 16)
            sp.wait_ge(pad_done, 16)

        @block.scalar
        def _(act):
            act.sem_inc(e_done, 2)
            act.wait_ge(par_step, EXP_STEPS + 1)
            act.activation(w[:, 1], res[:, 0], ACT.Exp).then_inc(act_par, 1)
            act.activation(w[:, 2], res[:, 0], ACT.Tanh, scale=0.5).then_inc(act_par, 1)
            act.wait_ge(par_step, EXP_STEPS + 10)
            act.activation(w[:, 3], w[:, 11], ACT.Sin).then_inc(act_par, 1)
            act.activation(w[:, 4], w[:, 11], ACT.Sin, scale=0.5).then_inc(act_par, 1)
            with act.Fori(0, G // 2) as i:
                for p in range(2):
                    act.wait_ge(earg_ready, 2 * i + p + 1)
                    act.activation(sh["mag"][:, bass.ds((2 * i + p) * GQ, GQ), :], earg[:, p], ACT.Exp).then_inc(e_done, 1)

        @block.tensor
        def _(pe):
            pe.wait_ge(const_in, 16)
            pe.wait_ge(par_step, EXP_STEPS + 43)
            for k in range(6):
                last = pe.transpose(ps[:, k, :], res[:, k, :], ident[0:Q, 0:Q])
            last.then_inc(turned, 1)

        @block.gpsimd
        def _(pool):
            pool.memset(zeros[:], 0.0).then_inc(cst, 1)
            with pool.Fori(0, B // 2) as i:
                for p in range(2):
                    pool.wait_ge(var_ready, 2 * i + p + 2)
                    pool.tensor_tensor(rstd[:, p], small[:, p, 4], minus_half[:], ALU.pow).then_inc(rstd_ready, 1)
            pool.wait_ge(par_ready, 1)
            with pool.Fori(0, G // 2) as i:
                for p in range(2):
                    pool.wait_ge(e_done, 2 * i + p + 1)
                    alpha = sh["modes"][:, 0, bass.ds((2 * i + p) * GQ, GQ)].unsqueeze(2).broadcast_to([P, GQ, T])
                    pool.tensor_tensor(earg[:, p], tcol.unsqueeze(1).broadcast_to([P, GQ, T]), alpha,
                                       ALU.mult).then_inc(earg_ready, 1)

        @block.vector
        def _(dve):
            steps = [0]

            def step(ins):
                steps[0] += 1
                ins.then_inc(par_step, 1)
                dve.wait_ge(par_step, steps[0])

            dve.sem_inc(x_free, 2)
            dve.memset(minus_half[:], -0.5).then_inc(var_ready, 1)
            dve.wait_ge(par_in, 80)
            tt, ts, stt = dve.tensor_tensor, dve.tensor_scalar, dve.scalar_tensor_tensor
            k_, r_, p_ = ex[:, 0], ex[:, 1], ex[:, 2]
            step(ts(logs[:], logs[:], -87.0, 88.0, ALU.max, ALU.min))
            step(ts(k_, logs[:], 1.4426950408889634, MAGIC, ALU.mult, ALU.add))
            step(ts(ex[:, 3], k_, MAGIC, None, ALU.subtract))
            step(stt(out=r_, in0=ex[:, 3], scalar=-LN2_HI, in1=logs[:], op0=ALU.mult, op1=ALU.add))
            step(stt(out=r_, in0=ex[:, 3], scalar=-LN2_LO, in1=r_, op0=ALU.mult, op1=ALU.add))
            step(ts(p_, r_, 1.0 / 5040, None, ALU.mult))
            for c in (1.0 / 720, 1.0 / 120, 1.0 / 24, 1.0 / 6, 0.5, 1.0):
                step(stt(out=p_, in0=p_, scalar=c, in1=r_, op0=ALU.add, op1=ALU.mult))
            step(ts(p_, p_, 1.0, None, ALU.add))
            step(ts(ex[:, 3].bitcast(I32), k_.bitcast(I32), 23, None, ALU.logical_shift_left))
            step(tt(ex[:, 4].bitcast(I32), p_.bitcast(I32), ex[:, 3].bitcast(I32), ALU.add))
            ea, aim, cre, cim = ex[:, 4, 0:P], par[:, 0, :], par[:, 1, :], par[:, 2, :]
            dtb = ex[:, 4, P:P + J].unsqueeze(2).broadcast_to([Q, J, N])

            def jn(ap):
                return ap.rearrange("q (j n) -> q j n", j=J)

            step(stt(out=jn(res[:, 0]), in0=jn(ea), scalar=-1.0, in1=dtb, op0=ALU.mult, op1=ALU.mult))
            step(tt(jn(w[:, 5]), jn(aim), dtb, ALU.mult))
            step(ts(w[:, 6], w[:, 5], INV_2PI, MAGIC, ALU.mult, ALU.add))
            step(ts(w[:, 7], w[:, 6], MAGIC, None, ALU.subtract))
            step(stt(out=w[:, 8], in0=w[:, 7], scalar=-PI_HI, in1=w[:, 5], op0=ALU.mult, op1=ALU.add))
            step(stt(out=w[:, 9], in0=w[:, 7], scalar=-PI_LO, in1=w[:, 8], op0=ALU.mult, op1=ALU.add))
            step(ts(w[:, 10], w[:, 9], 0.0, 2.0, ALU.is_ge, ALU.mult))
            step(ts(w[:, 10], w[:, 10], 1.0, None, ALU.subtract))
            step(tt(w[:, 11], w[:, 9], w[:, 10], ALU.mult))
            step(ts(w[:, 11], w[:, 11], 3.141592, None, ALU.min))
            sgn = w[:, 10]
            step(ts(res[:, 1], w[:, 11], INV_2PI, None, ALU.mult))
            step(tt(w[:, 12], aim, sgn, ALU.mult))
            step(tt(w[:, 13], cim, sgn, ALU.mult))
            dve.wait_ge(act_par, 4)
            e1, th, sn, hs, ai, ci = w[:, 1], w[:, 2], w[:, 3], w[:, 4], w[:, 12], w[:, 13]
            step(stt(out=w[:, 14], in0=e1, scalar=1.0, in1=th, op0=ALU.add, op1=ALU.mult))
            step(stt(out=w[:, 15], in0=hs, scalar=2.0, in1=hs, op0=ALU.mult, op1=ALU.mult))
            step(tt(w[:, 16], e1, w[:, 15], ALU.mult))
            step(tt(w[:, 17], w[:, 14], w[:, 16], ALU.subtract))
            step(tt(w[:, 18], e1, sn, ALU.mult))
            step(tt(w[:, 16], e1, w[:, 16], ALU.subtract))
            step(tt(w[:, 19], ea, ea, ALU.mult))
            step(tt(w[:, 20], ai, ai, ALU.mult))
            step(tt(w[:, 19], w[:, 19], w[:, 20], ALU.add))
            step(dve.reciprocal(w[:, 20], w[:, 19]))
            nr, ni = w[:, 17], w[:, 18]
            step(tt(w[:, 21], nr, ea, ALU.mult))
            step(tt(w[:, 22], ni, ai, ALU.mult))
            step(tt(w[:, 21], w[:, 22], w[:, 21], ALU.subtract))
            step(tt(w[:, 22], ni, ea, ALU.mult))
            step(tt(w[:, 23], nr, ai, ALU.mult))
            step(stt(out=w[:, 22], in0=w[:, 22], scalar=-1.0, in1=w[:, 23], op0=ALU.mult, op1=ALU.subtract))
            step(stt(out=w[:, 21], in0=w[:, 21], scalar=2.0, in1=w[:, 20], op0=ALU.mult, op1=ALU.mult))
            step(stt(out=w[:, 22], in0=w[:, 22], scalar=2.0, in1=w[:, 20], op0=ALU.mult, op1=ALU.mult))

            def cmul(outr, outi, ar, ai_, br, bi):
                dve_t = w[:, 23]
                step(tt(dve_t, ai_, bi, ALU.mult))
                step(tt(outr, ar, br, ALU.mult))
                step(tt(outr, outr, dve_t, ALU.subtract))
                step(tt(dve_t, ai_, br, ALU.mult))
                step(tt(outi, ar, bi, ALU.mult))
                step(tt(outi, outi, dve_t, ALU.add))

            cmul(res[:, 2], res[:, 3], cre, ci, w[:, 21], w[:, 22])
            cmul(res[:, 4], res[:, 5], res[:, 2], res[:, 3], w[:, 16], ni)
            dve.wait_ge(turned, 1)
            dve.tensor_copy(sh["modes"][:], ps[:]).then_inc(par_ready, 1)

            with dve.Fori(0, B // 2) as i:
                for p in range(2):
                    b = 2 * i + p
                    dve.wait_ge(x_in[p], 16 * i + 16)
                    for c in range(C):
                        last = dve.bn_stats(stats[:, p, c, :], xraw[:, p, c, :])
                    last.then_inc(stat_step, 1)
                    dve.wait_ge(stat_step, 7 * b + 1)
                    s = [stats[:, p, :, k] for k in range(6)]
                    tt(small[:, p, 0], s[1], s[4], ALU.add).then_inc(stat_step, 1)
                    tt(small[:, p, 1], s[1], s[4], ALU.subtract).then_inc(stat_step, 1)
                    tt(small[:, p, 2], s[2], s[5], ALU.add).then_inc(stat_step, 1)
                    dve.wait_ge(stat_step, 7 * b + 4)
                    ts(small[:, p, 5], small[:, p, 0], 0.5, None, ALU.mult).then_inc(stat_step, 1)
                    stt(out=small[:, p, 3], in0=small[:, p, 1], scalar=0.25, in1=small[:, p, 1],
                        op0=ALU.mult, op1=ALU.mult).then_inc(stat_step, 1)
                    ts(small[:, p, 2], small[:, p, 2], 1.0 / D, EPS, ALU.mult, ALU.add).then_inc(stat_step, 1)
                    dve.wait_ge(stat_step, 7 * b + 7)
                    tt(small[:, p, 4], small[:, p, 2], small[:, p, 3], ALU.add).then_inc(var_ready, 1)
                for p in range(2):
                    b = 2 * i + p
                    dve.wait_ge(rstd_ready, b + 1)
                    for c in range(C):
                        last = ts(sh["xn"][:, :, bass.ds(c * B + b, 1)].rearrange("p d o -> p (d o)"), xraw[:, p, c, :], small[:, p, 5, c:c + 1],
                                  rstd[:, p, c:c + 1], ALU.subtract, ALU.mult)
                    last.then_inc(x_free, 1)
            assert steps[0] == EXP_STEPS + 43, steps[0]


def mixer_groups(nc, io, sh):
    with ExitStack() as ctx:
        def sb(name, shape, dt=F32):
            return ctx.enter_context(nc.sbuf_tensor(name, shape, dt))

        def psum(name, shape, dt=F32):
            return ctx.enter_context(nc.psum_tensor(name, shape, dt))

        def sem(name):
            return ctx.enter_context(nc.semaphore(name))

        turns = sb("turns", [P, GQ, T])
        rounded = sb("rounded", [P, GQ, T])
        frac = sb("frac", [P, GQ, T])
        sine = sb("sine", [P, GQ, T])
        cosine = sb("cosine", [P, GQ, T])
        table = sb("table", [P, 2, 2, GQ, T])
        carry = sb("carry", [P, 2, GQ, 2])
        tin = sb("tin", [P, GQ, 2, P])
        weights = sb("weights", [P, 2, 2, GQ, GC])
        ksb = sb("ksb", [GC, P])
        toep = sb("toep", [P, GC, P])
        xg = sb("xg", [P, 2, GC, CB])
        z = sb("z", [P, GQ, 2, SB])
        za = sb("za", [P, GQ, 2, SB])
        zb = sb("zb", [P, GQ, 2, SB])
        dd = sb("dd", [P, GQ, 2])
        gl = sb("gl", [P, J, GQ, CB])
        half_pi = sb("half_pi", [P, 1])
        psY = psum("psY", [P, J, GQ, CB])
        psZ = psum("psZ", [P, 2, GQ // 2, 2, CB])
        psT = psum("psT", [P, 4, P])
        psK = psum("psK", [P, 512])

        cst = sem("cst_b")
        frac_step, trig_step, table_step, carry_step = (
            sem("frac_step"), sem("trig_step"), sem("table_step"), sem("carry_step"))
        w_ready, x_staged, k_done, k_copied, k_stored, toep_in, toep_used = (
            sem("w_ready"), sem("x_staged"), sem("k_done"), sem("k_copied"), sem("k_stored"), sem("toep_in"),
            sem("toep_used"))
        turned, tin_ready, z_ready, z_step, rec_step, y_ready = (
            sem("turned_b"), sem("tin_ready"), sem("z_ready"), sem("z_step"), sem("rec_step"),
            sem("y_ready"))
        gelu_done, hi_done, lo_done = sem("gelu_done"), sem("hi_done"), sem("lo_done")
        GL = J

        ident = sh["const"][:, C_ID:C_ID + P]
        tcol = sh["const"][:, C_POW:C_POW + T]
        mask = sh["const"][:, C_MASK:C_MASK + GQ * GC].rearrange("p (q m) -> p q m", q=GQ)
        y16 = sh["xn"][:].bitcast(F16).rearrange("p d (k c) -> p d k c", k=2)

        def mode(k, g):
            return sh["modes"][:, k, bass.ds(g * GQ, GQ)]

        def over(ap, *shape):
            for _ in shape:
                ap = ap.unsqueeze(len(ap.shape))
            return ap.broadcast_to([P, GQ, *shape])

        def groups(eng, body):
            body(0, 0, False)
            with eng.Fori(0, G // 2 - 1) as i:
                body(2 * i + 1, 1, False)
                body(2 * i + 2, 0, False)
            body(G - 1, 1, True)

        block = ctx.enter_context(nc.Block())

        @block.sync
        def _(sp):
            for g in range(G):
                sp.wait_ge(k_copied, g + 2)
                sp.dma_start(io["kpad"][g * GC:(g + 1) * GC, 0:P], ksb[:]).then_inc(k_stored, 16)
                sp.wait_ge(k_stored, 16 * g + 16)
                sp.wait_ge(toep_used, g + 1)
                src = bass.AP(io["kpad"].tensor, g * (GC * 2 * P), [[1, P], [2 * P, GC], [1, P]])
                sp.dma_start(toep[:], src).then_inc(toep_in, 16)

        @block.gpsimd
        def _(pool):
            def feed(g, p):
                if not (isinstance(g, int) and g < 2):
                    pool.wait_ge(k_done, g - 1)
                for k in range(2):
                    pool.tensor_tensor(weights[:, p, k], mask, over(mode(2 + k, g), GC), ALU.mult).then_inc(w_ready, 1)

            pool.memset(half_pi[:], PI / 2).then_inc(cst, 1)
            feed(0, 0)
            feed(1, 1)
            with pool.Fori(0, G // 2 - 1) as i:
                for p in range(2):
                    feed(2 * i + p + 2, p)

        @block.scalar
        def _(act):
            def trig(g):
                act.wait_ge(frac_step, 3 * g + 3)
                if not isinstance(g, int) or g > 0:
                    act.wait_ge(table_step, 2 * g)
                act.activation(sine[:], frac[:], ACT.Sin, scale=TWO_PI).then_inc(trig_step, 1)
                act.activation(cosine[:], frac[:], ACT.Abs).then_inc(trig_step, 1)
                act.wait_ge(trig_step, 3 * g + 2)
                act.activation(cosine[:], cosine[:], ACT.Sin, scale=-TWO_PI, bias=half_pi[:]).then_inc(trig_step, 1)

            def evacuate(g):
                if not isinstance(g, int) or g > 0:
                    act.wait_ge(z_ready, 2 * g)
                for k in range(4):
                    act.wait_ge(turned, 4 * g + k + 1)
                    act.activation(tin[:, 2 * k:2 * k + 2].rearrange("p q k t -> p (q k) t"), psT[:],
                                   ACT.Copy).then_inc(tin_ready, 1)
                act.wait_ge(k_done, g + 1)
                if not isinstance(g, int) or g > 0:
                    act.wait_ge(k_stored, 16 * g)
                act.activation(ksb[:], psK[0:GC, 0:P], ACT.Copy).then_inc(k_copied, 1)

            def stage(g, p):
                if not isinstance(g, int) or g > 0:
                    act.wait_ge(y_ready, J * g)
                act.activation(xg[:, p], sh["xn"][:, bass.ds(g * GC, GC), :], ACT.Copy).then_inc(x_staged, 1)

            def gelu(g):
                for j in range(J):
                    act.wait_ge(y_ready, J * g + j + 1 + J)
                    act.wait_ge(lo_done, J * g + j + 1)
                    act.activation(gl[:, j], psY[:, j], ACT.Gelu).then_inc(gelu_done, 1)
                for j in range(J):
                    act.wait_ge(gelu_done, J * g + j + 1 + J)
                    dst = y16[:, bass.ds(g * GC, GC), 0, :].rearrange("p (q j) c -> p j q c", j=J)[:, j]
                    act.activation(dst, gl[:, j], ACT.Copy, scale=Y_SCALE).then_inc(hi_done, 1)

            def body(g, p, last):
                if not last:
                    trig(g + 1)
                    stage(g + 1, 1 - p)
                    evacuate(g + 1)
                gelu(g)

            act.sem_inc(tin_ready, 1)
            act.sem_inc(k_copied, 1)
            act.sem_inc(gelu_done, J)
            act.wait_ge(cst, 1)
            trig(0)
            stage(0, 0)
            evacuate(0)
            groups(act, body)

        @block.tensor
        def _(pe):
            def feed(g, p):
                pe.wait_ge(table_step, 2 * g + 2)
                for k in range(4):
                    pe.wait_ge(tin_ready, 4 * g + k + 1)
                    for n in range(4):
                        last = pe.transpose(psT[:, n], table[:, p, n % 2, 2 * k + n // 2, 0:P], ident)
                    last.then_inc(turned, 1)
                pe.wait_ge(w_ready, 2 * g + 2)
                pe.wait_ge(k_copied, g + 1)
                for q in range(GQ):
                    for k in range(2):
                        last = pe.matmul(psK[0:GC, 0:P], weights[:, p, k, q], table[:, p, k, q, 0:P],
                                         start=(q == 0 and k == 0), stop=(q == GQ - 1 and k == 1))
                last.then_inc(k_done, 1)
                pe.wait_ge(x_staged, g + 1)
                pe.wait_ge(tin_ready, 4 * g + 5)
                for h in range(2):
                    if not isinstance(g, int) or g > 0:
                        pe.wait_ge(z_step, 8 * g - 3 + 3 * h)
                    for q in range(GQ // 2):
                        for k in range(2):
                            for j in range(J):
                                qq = h * (GQ // 2) + q
                                last = pe.matmul(psZ[N * j:N * j + N, h, q, k, 0:SB],
                                                 tin[:, qq, k, N * j:N * j + N],
                                                 xg[:, p, J * qq + j, 0:SB], start=True, stop=True)
                    last.then_inc(z_ready, 1)

            def body(g, p, last_group):
                if not last_group:
                    feed(g + 1, 1 - p)
                pe.wait_ge(toep_in, 16 * g + 16)
                for j in range(J):
                    pe.wait_ge(gelu_done, J * g + j + 1)
                    for q in range(GQ):
                        last = pe.matmul(psY[:, j, q], toep[:, J * q + j], xg[:, p, J * q + j],
                                         start=(q == 0), stop=False, skip_group_check=True)
                last.then_inc(toep_used, 1)
                pe.wait_ge(rec_step, 24 * g + 24)
                for q in range(GQ):
                    for k in range(2):
                        for j in range(J):
                            last = pe.matmul(psY[:, j, q, B:CB], table[N * j:N * j + N, p, k, q, 0:P],
                                             z[N * j:N * j + N, q, k], start=False, stop=(k == 1),
                                             skip_group_check=True)
                            if q == GQ - 1 and k == 1:
                                last.then_inc(y_ready, 1)

            pe.sem_inc(toep_used, 1)
            pe.sem_inc(y_ready, J)
            feed(0, 0)
            groups(pe, body)

        @block.vector
        def _(dve):
            tt, ts, stt = dve.tensor_tensor, dve.tensor_scalar, dve.scalar_tensor_tensor

            def phases(g):
                tt(turns[:], tcol.unsqueeze(1).broadcast_to([P, GQ, T]), over(mode(1, g), T),
                   ALU.mult).then_inc(frac_step, 1)
                dve.wait_ge(frac_step, 3 * g + 1)
                ts(rounded[:], turns[:], MAGIC, None, ALU.add).then_inc(frac_step, 1)
                dve.wait_ge(frac_step, 3 * g + 2)
                if not isinstance(g, int) or g > 0:
                    dve.wait_ge(trig_step, 3 * g - 1)
                stt(out=frac[:], in0=rounded[:], scalar=MAGIC, in1=turns[:], op0=ALU.subtract,
                    op1=ALU.subtract).then_inc(frac_step, 1)

            def tables(g, p):
                dve.wait_ge(trig_step, 3 * g + 3)
                if not isinstance(g, int) or g > 0:
                    dve.wait_ge(y_ready, J * g)
                mag = sh["mag"][:, bass.ds(g * GQ, GQ), :]
                tt(table[:, p, 0], cosine[:], mag, ALU.mult).then_inc(table_step, 1)
                tt(table[:, p, 1], sine[:], mag, ALU.mult).then_inc(table_step, 1)
                dve.wait_ge(table_step, 2 * g + 2)
                last_power = table[:, p, 1, :, P:P + 1]
                ts(carry[:, p, :, 0:1], last_power, 1.0, None, ALU.mult).then_inc(carry_step, 1)
                ts(carry[:, p, :, 1:2], last_power, -1.0, None, ALU.mult).then_inc(carry_step, 1)

            def states(g, p):
                ts(dd[:, :, 0:1], mode(4, g).unsqueeze(2), 1.0, None, ALU.mult).then_inc(z_step, 1)
                ts(dd[:, :, 1:2], mode(4, g).unsqueeze(2), -1.0, None, ALU.mult).then_inc(z_step, 1)
                dve.wait_ge(z_step, 8 * g + 2)
                half = GQ // 2
                for h in range(2):
                    rows = slice(h * half, h * half + half)
                    dve.wait_ge(z_ready, 2 * g + h + 1)
                    zp = psZ[:, h, :, :, 0:SB]
                    tt(za[:, rows], zp, dd[:, rows].unsqueeze(3).broadcast_to([P, half, 2, SB]), ALU.mult)\
                        .then_inc(z_step, 1)
                    di = sh["modes"][:, 5, bass.ds(g * GQ + h * half, half)]
                    tt(zb[:, rows], psZ[:, h, :, ::-1, 0:SB],
                       di.unsqueeze(2).unsqueeze(3).broadcast_to([P, half, 2, SB]), ALU.mult)\
                        .then_inc(z_step, 1)
                    dve.wait_ge(z_step, 8 * g + 4 + 3 * h)
                    dve.wait_ge(y_ready, J * g + J)
                    tt(z[:, rows], za[:, rows], zb[:, rows], ALU.add).then_inc(z_step, 1)
                dve.wait_ge(z_step, 8 * g + 8)
                dve.wait_ge(carry_step, 2 * g + 2)
                zc = z[:].rearrange("p q k (c b) -> p q k c b", b=B)
                a4 = za[:].rearrange("p q k (c b) -> p q k c b", b=B)
                b4 = zb[:].rearrange("p q k (c b) -> p q k c b", b=B)
                re = table[:, p, 0, :, P:P + 1].unsqueeze(3).broadcast_to([P, GQ, 2, B])
                im = carry[:, p].unsqueeze(3).broadcast_to([P, GQ, 2, B])
                n = 24 * g
                for c in range(1, C - 1):
                    tt(a4[:, :, :, c], zc[:, :, :, c - 1], re, ALU.mult).then_inc(rec_step, 1)
                    tt(b4[:, :, :, c], zc[:, :, ::-1, c - 1], im, ALU.mult).then_inc(rec_step, 1)
                    dve.wait_ge(rec_step, n + 4 * c - 2)
                    tt(a4[:, :, :, c], a4[:, :, :, c], b4[:, :, :, c], ALU.add).then_inc(rec_step, 1)
                    dve.wait_ge(rec_step, n + 4 * c - 1)
                    tt(zc[:, :, :, c], zc[:, :, :, c], a4[:, :, :, c], ALU.add).then_inc(rec_step, 1)
                    dve.wait_ge(rec_step, n + 4 * c)

            def remainders(g):
                for j in range(J):
                    dve.wait_ge(hi_done, J * g + j + 1)
                    part = y16[:, bass.ds(g * GC, GC)].rearrange("p (q j) k c -> p j q k c", j=J)[:, j]
                    stt(out=part[:, :, 1], in0=gl[:, j], scalar=Y_SCALE, in1=part[:, :, 0],
                        op0=ALU.mult, op1=ALU.subtract).then_inc(lo_done, 1)

            def body(g, p, last):
                if not last:
                    phases(g + 1)
                if not isinstance(g, int) or g > 0:
                    remainders(g - 1)
                if not last:
                    tables(g + 1, 1 - p)
                states(g, p)

            dve.sem_inc(lo_done, GL)
            phases(0)
            tables(0, 0)
            groups(dve, body)
            remainders(G - 1)


def feed_forward(nc, io, sh):
    S = B * L // (ST * P)
    PAIRS = ST // 2
    LN_STEPS = 10
    TERMS = ((0, 0), (0, 1), (1, 0))
    with ExitStack() as ctx:
        def sb(name, shape, dt=F32):
            return ctx.enter_context(nc.sbuf_tensor(name, shape, dt))

        def psum(name, shape, dt=F32):
            return ctx.enter_context(nc.psum_tensor(name, shape, dt))

        def sem(name):
            return ctx.enter_context(nc.semaphore(name))

        wp_raw = sb("wp_raw", [P, KD, D])
        wp = sb("wp", [P, 2, KD, D], F16)
        w1_raw = sb("w1_raw", [P, KD, F])
        w2_raw = sb("w2_raw", [P, KF, D])
        w1 = sb("w1", [P, 2, 2, KD, F], F16)
        w2 = sb("w2", [P, 2, 2, KF, D], F16)
        bias = sb("bias", [P, D])
        b1_raw = sb("b1_raw", [E * KF, P])
        b1 = sb("b1", [P, E * KF])
        b1_now = sb("b1_now", [P, 2, KF])
        b2 = sb("b2", [P, E, D])
        id16 = sb("id16", [P, P], F16)
        rev16 = sb("rev16", [P, P], F16)
        xres = sb("xres", [P, 4, ST, D])
        yT = sb("yT", [P, 2, KD, 2, P], F16)
        z = sb("zproj", [P, ST, D])
        hin = sb("hin", [P, ST, D])
        hin16 = sb("hin16", [P, 2, ST, D], F16)
        hT = sb("hT", [P, 2, 2, KD, ST, P], F16)
        a32 = sb("a32", [P, 2, ST * P])
        a16 = sb("a16", [P, 2, KF, ST * P], F16)
        ff = sb("ff", [P, 2, ST, D])
        NA, NX, NB = range(3)
        stats = sb("stats_c", [P, 3, ST, 6])
        small = sb("small_c", [P, 3, 4, ST])
        var = sb("var", [P, 3, ST])
        rstd = sb("rstd_c", [P, 3, ST])
        nmr = sb("nmr", [P, 3, ST])
        minus_half = sb("minus_half_c", [P, ST])
        ps_yT = psum("ps_yT", [P, 2, KD, 2, P])
        ps_z = psum("ps_z", [P, 2, D])
        ps_hT = psum("ps_hT", [P, 2, KD, 2, P], F16)
        ps_a = psum("ps_a", [P, 2, ST * P])
        ps_f = psum("ps_f", [P, PAIRS, 2, D])

        start_in, w1_in, w2_in, x_in, stored = (
            sem("start_in"), sem("w1_in"), sem("w2_in"), [sem(f"x_in_c{k}") for k in range(4)],
            [sem("stored0"), sem("stored1")])
        cst, b1_ready, id_done, turned_w, wp_hi, wp_lo, w1_hi, w1_lo, w2_hi, w2_lo = (
            sem("cst_c"), sem("b1_ready"), sem("id_done"), sem("turned_w"), sem("wp_hi"), sem("wp_lo"), sem("w1_hi"), sem("w1_lo"), sem("w2_hi"),
            sem("w2_lo"))
        yT_ready, yT_done, z_ready, hT_ready, hT_done = (
            sem("yT_ready"), sem("yT_done"), sem("z_ready_c"), sem("hT_ready"), sem("hT_done"))
        a_ready, a_hi, a_lo, f_ready = sem("a_ready"), sem("a_hi"), sem("a_lo"), sem("f_ready")
        ln_step, ln_var, ln_rstd, ln_nmr, ln_done = (
            [sem(f"{n}{k}") for k in range(3)] for n in ("ln_step", "ln_var", "ln_rstd", "ln_nmr", "ln_done"))
        x1_done, hin_hi, hin_lo, out_ready = sem("x1_done"), sem("hin_hi"), sem("hin_lo"), sem("out_ready")
        y16 = sh["xn"][:].bitcast(F16).rearrange("p d (k c) -> p d k c", k=2)
        ident = sh["const"][:, C_ID:C_ID + P]

        def windows(body):
            def run(eng):
                body(0, 0)
                with eng.Fori(0, (S - 4) // 4) as i:
                    for k in range(4):
                        body(4 * i + k + 1, (k + 1) % 4)
                for s in range(S - 3, S):
                    body(s, s % 4)
            return run

        def known(s, least):
            return not isinstance(s, int) or s >= least

        def there(s):
            return not isinstance(s, int) or s < S

        def expert(s, k, ahead=0):
            if isinstance(s, int):
                return (s + ahead) // 2
            return (s - k) // 2 + (k + ahead) // 2

        block = ctx.enter_context(nc.Block())

        @block.sync
        def _(sp):
            def load_w1(e):
                sp.dma_start(w1_raw[:], io["w1"][bass.ds(e, 1)].rearrange("o (k p) f -> p (o k) f", p=P)).then_inc(w1_in, 16)

            def load_w2(e):
                sp.dma_start(w2_raw[:], io["w2"][bass.ds(e, 1)].rearrange("o (k p) d -> p (o k) d", p=P)).then_inc(w2_in, 16)

            def load_x(s, k):
                sp.dma_start(xres[:, k], io["x"].rearrange("b (u t p) d -> (b u) p t d", p=P, t=ST)[bass.ds(s, 1)]
                             .rearrange("o p t d -> p (o t) d")).then_inc(x_in[k], 16)

            def store(s, k):
                sp.wait_ge(out_ready, s + 1)
                sp.dma_start(io["out"].rearrange("b (u t p) d -> (b u) p t d", p=P, t=ST)[bass.ds(s, 1)]
                             .rearrange("o p t d -> p (o t) d"), ff[:, k % 2]).then_inc(stored[k % 2], 16)

            sp.dma_start(wp_raw[:], io["W"].rearrange("(k p) d -> p k d", p=P)).then_inc(start_in, 16)
            sp.dma_start(b1_raw[:], io["b1"].rearrange("e (k p) -> (e k) p", p=P)).then_inc(start_in, 16)
            sp.dma_start(bias[:], io["b"].partition_broadcast(P)).then_inc(start_in, 16)
            for e in range(E):
                sp.dma_start(b2[:, e], io["b2"][e].partition_broadcast(P)).then_inc(start_in, 16)
            load_x(0, 0)
            load_w1(0)
            load_w2(0)
            load_x(1, 1)
            load_x(2, 2)
            sp.wait_ge(w1_lo, 1)
            load_w1(1)

            def body(s, k):
                if known(s, 1):
                    store(s - 1, k - 1)
                if there(s + 3):
                    load_x(s + 3, (k + 3) % 4)
                e = expert(s, k)
                if k % 2 == 0 and (not isinstance(s, int) or e + 1 < E):
                    sp.wait_ge(w2_lo, e + 1)
                    load_w2(e + 1)
                if k % 2 == 1 and (not isinstance(s, int) or e + 2 < E):
                    sp.wait_ge(w1_lo, e + 2)
                    load_w1(e + 2)

            windows(body)(sp)
            store(S - 1, (S - 1) % 4)
            for p in range(2):
                sp.wait_ge(stored[p], 16 * (S // 2))

        @block.gpsimd
        def _(pool):
            pool.memset(minus_half[:], -0.5).then_inc(cst, 1)
            pool.wait_ge(cst, 1)

            def power(n, s):
                pool.wait_ge(ln_var[n], s + 1)
                pool.tensor_tensor(rstd[:, n], var[:, n], minus_half[:], ALU.pow).then_inc(ln_rstd[n], 1)
                pool.wait_ge(ln_rstd[n], s + 1)
                pool.tensor_tensor(nmr[:, n], small[:, n, 0], rstd[:, n], ALU.mult).then_inc(ln_nmr[n], 1)

            def residual(s, k):
                for t in range(ST):
                    last = pool.tensor_scalar(z[:, t], z[:, t], small[:, NA, 0, t:t + 1], rstd[:, NA, t:t + 1],
                                              ALU.add, ALU.mult)
                last.then_inc(ln_done[NA], 1)
                pool.wait_ge(ln_done[NA], s + 1)
                pool.wait_ge(x_in[k], 16 * (s // 4) + 16 if isinstance(s, int) else 4 * (s - k) + 16)
                pool.tensor_tensor(xres[:, k], xres[:, k], z[:], ALU.add).then_inc(x1_done, 1)

            def finish(s, k):
                pool.wait_ge(ln_done[NB], s + 1)
                pool.tensor_tensor(ff[:, k % 2], ff[:, k % 2], xres[:, k], ALU.add).then_inc(out_ready, 1)

            def body(s, k):
                if there(s + 1):
                    power(NA, s + 1)
                    residual(s + 1, (k + 1) % 4)
                if known(s, 1):
                    power(NB, s - 1)
                if there(s + 1):
                    power(NX, s + 1)
                if known(s, 1):
                    finish(s - 1, (k - 1) % 4)

            power(NA, 0)
            residual(0, 0)
            power(NX, 0)
            windows(body)(pool)
            power(NB, S - 1)
            finish(S - 1, (S - 1) % 4)

        @block.scalar
        def _(act):
            def evacuate_yT(s, t):
                act.wait_ge(yT_ready, ST * s + t + 1)
                if known(s, 1) or t >= 2:
                    act.wait_ge(z_ready, PAIRS * s + t // 2)
                act.activation(yT[:, t % 2], ps_yT[:, t % 2], ACT.Copy).then_inc(yT_done, 1)

            def normalise(n, s, out, data):
                act.wait_ge(ln_nmr[n], s + 1)
                for t in range(ST):
                    last = act.activation(out[:, t], data[:, t], ACT.Identity, scale=rstd[:, n, t:t + 1],
                                          bias=nmr[:, n, t:t + 1])
                last.then_inc(ln_done[n], 1)

            def hidden(s, k, f):
                act.wait_ge(a_ready, KF * s + f + 1)
                if k % 2 == 0 and f == 0:
                    act.wait_ge(b1_ready, expert(s, k) + 1)
                b = b1_now[:, k // 2, f:f + 1]
                act.activation(a16[:, 0, f], ps_a[:, f % 2], ACT.Gelu_apprx_tanh, scale=1.0 / W_SCALE, bias=b)
                if known(s, 1) or f >= 2:
                    act.wait_ge(a_lo, KF * s + f - 1)
                act.activation(a32[:, f % 2], ps_a[:, f % 2], ACT.Gelu_apprx_tanh, scale=1.0 / W_SCALE,
                               bias=b).then_inc(a_hi, 1)

            def split_w1(e, ep):
                act.wait_ge(w1_in, 16 * e + 16)
                act.activation(w1[:, ep, 0], w1_raw[:], ACT.Copy, scale=W_SCALE).then_inc(w1_hi, 1)

            def split_w2(e, ep):
                act.wait_ge(w2_in, 16 * e + 16)
                act.activation(w2[:, ep, 0], w2_raw[:], ACT.Copy, scale=W_SCALE).then_inc(w2_hi, 1)

            def body(s, k):
                for f in range(KF):
                    hidden(s, k, f)
                if there(s + 2):
                    evacuate_yT(s + 2, 0)
                    evacuate_yT(s + 2, 1)
                if known(s, 1):
                    normalise(NB, s - 1, ff[:, (k - 1) % 2], ff[:, (k - 1) % 2])
                if there(s + 1):
                    normalise(NX, s + 1, hin, xres[:, (k + 1) % 4])
                if there(s + 2):
                    evacuate_yT(s + 2, 2)
                    evacuate_yT(s + 2, 3)
                e = expert(s, k)
                if k % 2 == 0 and (not isinstance(s, int) or e + 1 < E):
                    split_w1(e + 1, (k // 2 + 1) % 2)
                if k % 2 == 1 and (not isinstance(s, int) or e + 1 < E):
                    split_w2(e + 1, (k // 2 + 1) % 2)

            act.wait_ge(turned_w, 1)
            act.activation(wp[:, 0], ps_a[:, 0].rearrange("p (k e) -> p k e", k=KD), ACT.Copy, scale=W_SCALE)\
                .then_inc(wp_hi, 1)
            for t in range(ST):
                evacuate_yT(0, t)
            split_w1(0, 0)
            split_w2(0, 0)
            normalise(NX, 0, hin, xres[:, 0])
            for t in range(ST):
                evacuate_yT(1, t)
            windows(body)(act)
            normalise(NB, S - 1, ff[:, (S - 1) % 2], ff[:, (S - 1) % 2])

        @block.tensor
        def _(pe):
            def turn_y(s, k, t):
                if known(s, 1) or t >= 2:
                    pe.wait_ge(yT_done, ST * s + t - 1)
                e = expert(s, k)
                c = (k % 2) * ST + t
                for h in range(KD):
                    for part in range(2):
                        tile = y16[:, h * P:(h + 1) * P, part, bass.ds(c * B + e, 1)].rearrange("p d o -> p (d o)")
                        last = pe.matmul(ps_yT[:, t % 2, h, part], tile, rev16[:], start=True, stop=True)
                last.then_inc(yT_ready, 1)

            def project(s, r):
                if known(s, 1) or r == 1:
                    pe.wait_ge(ln_step[NA], LN_STEPS * s + 1 if r == 1 else LN_STEPS * s - LN_STEPS + 3)
                for t in range(2):
                    pe.wait_ge(yT_done, ST * s + 2 * r + t + 1)
                    n = 0
                    for wk, yk in TERMS:
                        for h in range(KD):
                            last = pe.matmul(ps_z[:, t], yT[:, t, h, yk], wp[:, wk, h], start=(n == 0), stop=(n == 5))
                            n += 1
                last.then_inc(z_ready, 1)

            def turn_h(s, r):
                pe.wait_ge(hin_lo, s + 1)
                if known(s, 1) or r == 1:
                    pe.wait_ge(hT_done, PAIRS * s + r)
                for t in range(2):
                    for h in range(KD):
                        for part in range(2):
                            last = pe.transpose(ps_hT[:, t, h, part], hin16[:, part, 2 * r + t, h * P:(h + 1) * P], id16[:])
                last.then_inc(hT_ready, 1)

            def layer1(s, k, f):
                ep = k // 2
                if known(s, 1) or f >= 2:
                    pe.wait_ge(a_hi, KF * s + f - 1)
                n = 0
                for wk, xk in TERMS:
                    for h in range(KD):
                        last = pe.matmul(ps_a[:, f % 2], w1[:, ep, wk, h, f * P:(f + 1) * P],
                                         hT[:, k % 2, xk, h].rearrange("p t n -> p (t n)"), start=(n == 0), stop=(n == 5))
                        n += 1
                last.then_inc(a_ready, 1)

            def layer2(s, k, t):
                ep = k // 2
                if t % 2 == 0 and (known(s, 1)):
                    pe.wait_ge(ln_step[NB], LN_STEPS * s - LN_STEPS + t + 1)
                for f in range(KF):
                    if t == 0:
                        pe.wait_ge(a_lo, KF * s + f + 1)
                    for n, (wk, ak) in enumerate(TERMS):
                        last = pe.matmul(ps_f[:, t // 2, t % 2], a16[:, ak, f, t * P:(t + 1) * P], w2[:, ep, wk, f],
                                         start=(f == 0 and n == 0), stop=(f == KF - 1 and n == 2))
                if t % 2 == 1:
                    last.then_inc(f_ready, 1)

            def body(s, k):
                pe.wait_ge(hT_done, PAIRS * s + PAIRS)
                if k % 2 == 0:
                    pe.wait_ge(w1_lo, expert(s, k) + 1)
                for f in range(KF):
                    layer1(s, k, f)
                nxt, nk, far, fk = s + 1, (k + 1) % 4, s + 2, (k + 2) % 4
                if there(far):
                    turn_y(far, fk, 0)
                    turn_y(far, fk, 1)
                if k % 2 == 0:
                    pe.wait_ge(w2_lo, expert(s, k) + 1)
                layer2(s, k, 0)
                layer2(s, k, 1)
                if there(far):
                    project(far, 0)
                    turn_y(far, fk, 2)
                    turn_y(far, fk, 3)
                layer2(s, k, 2)
                if there(nxt):
                    turn_h(nxt, 0)
                layer2(s, k, 3)
                if there(nxt):
                    turn_h(nxt, 1)
                if there(far):
                    project(far, 1)

            pe.wait_ge(start_in, 16 * (3 + E))
            for h in range(KD):
                for k in range(KD):
                    last = pe.transpose(ps_a[:, 0, h * D + k * P:h * D + (k + 1) * P], wp_raw[:, k, h * P:(h + 1) * P], ident)
            last = pe.transpose(ps_a[:, 1, 0:E * KF], b1_raw[:], ident[0:E * KF, 0:E * KF])
            last.then_inc(turned_w, 1)
            pe.wait_ge(id_done, 2)
            turn_y(0, 0, 0)
            turn_y(0, 0, 1)
            pe.wait_ge(wp_lo, 2)
            project(0, 0)
            turn_y(0, 0, 2)
            turn_y(0, 0, 3)
            project(0, 1)
            turn_y(1, 1, 0)
            turn_y(1, 1, 1)
            turn_h(0, 0)
            project(1, 0)
            turn_y(1, 1, 2)
            turn_y(1, 1, 3)
            turn_h(0, 1)
            project(1, 1)
            windows(body)(pe)

        @block.vector
        def _(dve):
            tt, ts, stt = dve.tensor_tensor, dve.tensor_scalar, dve.scalar_tensor_tensor

            def biased(n, s, r, out, data, scale, b):
                stt(out=out[:, 2 * r:2 * r + 2], in0=data, scalar=scale, in1=b.unsqueeze(1).broadcast_to([P, 2, D]),
                    op0=ALU.mult, op1=ALU.add).then_inc(ln_step[n], 1)
                dve.wait_ge(ln_step[n], LN_STEPS * s + 2 * r + 1)
                for t in range(2 * r, 2 * r + 2):
                    last = dve.bn_stats(stats[:, n, t], out[:, t])
                last.then_inc(ln_step[n], 1)

            def variance(n, s):
                st = [stats[:, n, :, k] for k in range(6)]
                sm = [small[:, n, k] for k in range(4)]
                if known(s, 1):
                    dve.wait_ge(ln_nmr[n], s)
                dve.wait_ge(ln_step[n], LN_STEPS * s + 4)
                tt(sm[0], st[1], st[4], ALU.add).then_inc(ln_step[n], 1)
                tt(sm[1], st[1], st[4], ALU.subtract).then_inc(ln_step[n], 1)
                tt(sm[2], st[2], st[5], ALU.add).then_inc(ln_step[n], 1)
                dve.wait_ge(ln_step[n], LN_STEPS * s + 7)
                stt(out=sm[3], in0=sm[1], scalar=0.25, in1=sm[1], op0=ALU.mult, op1=ALU.mult).then_inc(ln_step[n], 1)
                ts(sm[2], sm[2], 1.0 / D, EPS, ALU.mult, ALU.add).then_inc(ln_step[n], 1)
                ts(sm[0], sm[0], -0.5, None, ALU.mult).then_inc(ln_step[n], 1)
                dve.wait_ge(ln_step[n], LN_STEPS * s + 10)
                tt(var[:, n], sm[2], sm[3], ALU.add).then_inc(ln_var[n], 1)

            def z_pair(s, r):
                dve.wait_ge(z_ready, PAIRS * s + r + 1)
                if r == 0 and known(s, 1):
                    dve.wait_ge(x1_done, s)
                biased(NA, s, r, z, ps_z[:], 1.0 / (Y_SCALE * W_SCALE), bias[:])

            def f_pair(s, k, r):
                dve.wait_ge(f_ready, PAIRS * s + r + 1)
                if r == 0 and known(s, 2):
                    dve.wait_ge(stored[k % 2], stored_count(s, k))
                e = expert(s, k)
                biased(NB, s, r, ff[:, k % 2], ps_f[:, r], 1.0 / W_SCALE, b2[:, bass.ds(e, 1)].rearrange("p o d -> p (o d)"))

            def stored_count(s, k):
                return 16 * (s // 2) if isinstance(s, int) else 8 * (s - k % 2)

            def x1_statistics(s, k):
                dve.wait_ge(x1_done, s + 1)
                for t in range(ST):
                    last = dve.bn_stats(stats[:, NX, t], xres[:, k, t])
                last.then_inc(ln_step[NX], 4)
                variance(NX, s)

            def split_h(s):
                dve.wait_ge(ln_done[NX], s + 1)
                if known(s, 1):
                    dve.wait_ge(hT_ready, PAIRS * s)
                ts(hin16[:, 0], hin[:], 1.0, None, ALU.mult).then_inc(hin_hi, 1)
                dve.wait_ge(hin_hi, s + 1)
                tt(hin16[:, 1], hin[:], hin16[:, 0], ALU.subtract).then_inc(hin_lo, 1)

            def evacuate_h(s, k, r):
                dve.wait_ge(hT_ready, PAIRS * s + r + 1)
                for h in range(KD):
                    last = dve.tensor_copy(
                        hT[:, k % 2, :, h, 2 * r:2 * r + 2], ps_hT[:, :, h].rearrange("p t k n -> p k t n"))
                last.then_inc(hT_done, 1)

            def lower(s, f):
                dve.wait_ge(a_hi, KF * s + f + 1)
                tt(a16[:, 1, f], a32[:, f % 2], a16[:, 0, f], ALU.subtract).then_inc(a_lo, 1)

            def split_w(e, ep, w, raw, hi, lo):
                dve.wait_ge(hi, e + 1)
                stt(out=w[:, ep, 1], in0=raw[:], scalar=W_SCALE, in1=w[:, ep, 0], op0=ALU.mult,
                    op1=ALU.subtract).then_inc(lo, 1)

            def next_b1(e, ep):
                ts(b1_now[:, ep], b1[:, bass.ds(e * KF, KF)], 1.0, None, ALU.mult).then_inc(b1_ready, 1)

            def body(s, k):
                nxt, nk, far, fk = s + 1, (k + 1) % 4, s + 2, (k + 2) % 4
                lower(s, 0)
                if there(nxt):
                    z_pair(nxt, 1)
                lower(s, 1)
                if there(nxt):
                    variance(NA, nxt)
                lower(s, 2)
                if known(s, 1):
                    f_pair(s - 1, (k - 1) % 4, 1)
                lower(s, 3)
                if known(s, 1):
                    variance(NB, s - 1)
                for f in range(4, KF):
                    lower(s, f)
                if there(nxt):
                    x1_statistics(nxt, nk)
                e = expert(s, k)
                if k % 2 == 0 and (not isinstance(s, int) or e + 1 < E):
                    split_w(e + 1, (k // 2 + 1) % 2, w1, w1_raw, w1_hi, w1_lo)
                if k % 2 == 1 and (not isinstance(s, int) or e + 1 < E):
                    split_w(e + 1, (k // 2 + 1) % 2, w2, w2_raw, w2_hi, w2_lo)
                    next_b1(e + 1, (k // 2 + 1) % 2)
                if there(nxt):
                    split_h(nxt)
                if there(far):
                    z_pair(far, 0)
                f_pair(s, k, 0)
                if there(nxt):
                    evacuate_h(nxt, nk, 0)
                    evacuate_h(nxt, nk, 1)

            ts(id16[:], ident, 1.0, None, ALU.mult).then_inc(id_done, 1)
            ts(rev16[:], sh["const"][:, C_REV:C_REV + P], 1.0, None, ALU.mult).then_inc(id_done, 1)
            dve.wait_ge(turned_w, 1)
            dve.tensor_copy(b1[:], ps_a[:, 1, 0:E * KF]).then_inc(wp_lo, 1)
            dve.wait_ge(wp_hi, 1)
            stt(out=wp[:, 1], in0=ps_a[:, 0].rearrange("p (k e) -> p k e", k=KD), scalar=W_SCALE, in1=wp[:, 0],
                op0=ALU.mult, op1=ALU.subtract).then_inc(wp_lo, 1)
            z_pair(0, 0)
            z_pair(0, 1)
            variance(NA, 0)
            dve.wait_ge(wp_lo, 2)
            next_b1(0, 0)
            split_w(0, 0, w1, w1_raw, w1_hi, w1_lo)
            split_w(0, 0, w2, w2_raw, w2_hi, w2_lo)
            x1_statistics(0, 0)
            split_h(0)
            evacuate_h(0, 0, 0)
            z_pair(1, 0)
            evacuate_h(0, 0, 1)
            windows(body)(dve)
            f_pair(S - 1, (S - 1) % 4, 1)
            variance(NB, S - 1)


def sandwich(nc, io):
    with ExitStack() as ctx:
        sh = {"const": ctx.enter_context(nc.sbuf_tensor("constants", [P, C_END], F32)),
              "xn": ctx.enter_context(nc.sbuf_tensor("xn", [P, D, CB], F32))}
        with ExitStack() as mixer:
            sh["mag"] = mixer.enter_context(nc.sbuf_tensor("magnitudes", [P, Q, T], F32))
            sh["modes"] = mixer.enter_context(nc.sbuf_tensor("modes", [P, 6, Q], F32))
            mixer_prologue(nc, io, sh)
            mixer_groups(nc, io, sh)
        feed_forward(nc, io, sh)


_INS = ["L0_attn_x", "L0_attn_log_dt", "L0_attn_log_A_real", "L0_attn_A_imag", "L0_attn_C_real", "L0_attn_C_imag",
        "L0_attn_W", "L0_attn_b", "L0_ffn_w1", "L0_ffn_b1", "L0_ffn_w2", "L0_ffn_b2"]


def kernel(**inputs):
    import numpy as _np
    import concourse.bacc as _bacc
    from concourse import mybir as _mybir
    from concourse.bass_utils import run_bass_kernel_spmd as _run

    nc = _bacc.Bacc("TRN2", target_bir_lowering=False, num_devices=1)
    arrays, io = {}, {}
    for name in _INS:
        a = _np.ascontiguousarray(inputs[name])
        arrays[f"in_{name}_dram"] = a
        io[name.split("_", 2)[2]] = nc.dram_tensor(
            f"in_{name}_dram", a.shape, _mybir.dt.from_np(a.dtype), kind="ExternalInput").ap()
    const = _np.zeros((P, C_END), _np.float32)
    const[:, C_ID:C_ID + P] = _np.eye(P)
    const[:, C_REV:C_REV + P] = _np.eye(P)[::-1]
    const[:, C_POW:C_POW + P] = _np.arange(P)[::-1]
    const[:, C_POW + P] = P
    mask = const[:, C_MASK:].reshape(P, GQ, GC)
    for q in range(GQ):
        for j in range(J):
            mask[j * N:(j + 1) * N, q, J * q + j] = 1.0
    arrays["in_const_dram"] = const
    io["const"] = nc.dram_tensor("in_const_dram", const.shape, _mybir.dt.float32, kind="ExternalInput").ap()
    io["kpad"] = nc.dram_tensor("kpad", [D, 2 * P], _mybir.dt.float32, kind="Internal").ap()
    io["out"] = nc.dram_tensor("out_0_dram", [B, L, D], _mybir.dt.float32, kind="ExternalOutput").ap()
    sandwich(nc, io)
    r = _run(nc, [arrays], core_ids=[0])
    return r.results[0]["out_0_dram"]
```

```python
from contextlib import ExitStack

import concourse.bass as bass
from concourse import mybir

F32 = mybir.dt.float32
F16 = mybir.dt.float16
I32 = mybir.dt.int32
ALU = mybir.AluOpType
ACT = mybir.ActivationFunctionType

P = 128
B, L, D = 8, 1024, 256
N = 32
E, F = 8, 1024
C = L // P
CB = C * B
SB = (C - 1) * B
J = P // N
Q = D // J
T = P + 1
GQ = 8
GC = GQ * J
G = Q // GQ
KD = D // P
KF = F // P
ST = 4
EPS = 1e-5
PI = 3.14159265358979
TWO_PI = 6.283185
INV_2PI = 0.15915494309189535
PI_HI, PI_LO = 6.28125, 0.0019353071795864769
LN2_HI, LN2_LO = 0.693359375, -2.12194440054690583e-4
EXP_STEPS = 15
MAGIC = 12582912.0
K_SCALE, W_SCALE = 64.0, 64.0
C_ID, C_REV, C_POW, C_MASK = 0, P, 2 * P, 2 * P + T
C_END = C_MASK + GQ * GC


def mixer_prologue(nc, io, sh):
    with ExitStack() as ctx:
        def sb(name, shape, dt=F32):
            return ctx.enter_context(nc.sbuf_tensor(name, shape, dt))

        def sem(name):
            return ctx.enter_context(nc.semaphore(name))

        par = sb("par", [Q, 3, P])
        logs = sb("logs", [Q, P + J])
        ex = sb("ex", [Q, 5, P + J])
        w = sb("w", [Q, 24, P])
        res = sb("res", [Q, 6, P])
        xraw = sb("xraw", [P, 2, C, D])
        stats = sb("stats", [P, 2, C, 6])
        small = sb("small", [P, 2, 6, C])
        minus_half = sb("minus_half", [P, C])
        rstd = sb("rstd", [P, 2, C])
        earg = sb("earg", [P, 2, GQ, T])
        zeros = sb("zeros", [P, KD, P, 2], F16)
        ps = ctx.enter_context(nc.psum_tensor("psP", [P, 6, Q], F32))

        par_in, x_in, const_in = sem("par_in"), [sem("x_in0"), sem("x_in1")], sem("const_in")
        x_free, stat_step, var_ready, rstd_ready, xn_step = (
            sem("x_free"), sem("stat_step"), sem("var_ready"), sem("rstd_ready"), sem("xn_step"))
        par_step, act_par, turned, par_ready = sem("par_step"), sem("act_par"), sem("turned"), sem("par_ready")
        cst, earg_ready, e_done, pad_done = sem("cst"), sem("earg_ready"), sem("e_done"), sem("pad_done")

        ident = sh["const"][:, C_ID:C_ID + P]
        tcol = sh["const"][:, C_POW:C_POW + T]
        block = ctx.enter_context(nc.Block())

        @block.sync
        def _(sp):
            sp.dma_start(logs[:, 0:P], io["log_A_real"].rearrange("(q j) n -> q (j n)", j=J)).then_inc(par_in, 16)
            for k, name in enumerate(("A_imag", "C_real", "C_imag")):
                sp.dma_start(par[:, k, :], io[name].rearrange("(q j) n -> q (j n)", j=J)).then_inc(par_in, 16)
            sp.dma_start(logs[:, P:P + J], io["log_dt"].rearrange("(q j) -> q j", j=J)).then_inc(par_in, 16)
            sp.dma_start(sh["const"][:], io["const"]).then_inc(const_in, 16)
            for b in range(B):
                sp.wait_ge(x_free, b + 1)
                sp.dma_start(xraw[:, b % 2], io["x"][b].rearrange("(c p) d -> p c d", p=P)).then_inc(x_in[b % 2], 16)
            sp.wait_ge(cst, 1)
            sp.dma_start(io["kpad"].rearrange("(h p) t k -> p h (t k)", p=P)[:, :, 2 * P:4 * P],
                         zeros[:].rearrange("p h t k -> p h (t k)")).then_inc(pad_done, 16)
            sp.wait_ge(pad_done, 16)

        @block.scalar
        def _(act):
            act.sem_inc(e_done, 2)
            act.wait_ge(par_step, EXP_STEPS + 1)
            act.activation(w[:, 1], res[:, 0], ACT.Exp).then_inc(act_par, 1)
            act.activation(w[:, 2], res[:, 0], ACT.Tanh, scale=0.5).then_inc(act_par, 1)
            act.wait_ge(par_step, EXP_STEPS + 10)
            act.activation(w[:, 3], w[:, 11], ACT.Sin).then_inc(act_par, 1)
            act.activation(w[:, 4], w[:, 11], ACT.Sin, scale=0.5).then_inc(act_par, 1)
            with act.Fori(0, G // 2) as i:
                for p in range(2):
                    act.wait_ge(earg_ready, 2 * i + p + 1)
                    act.activation(sh["mag"][:, bass.ds((2 * i + p) * GQ, GQ), :], earg[:, p], ACT.Exp).then_inc(e_done, 1)

        @block.tensor
        def _(pe):
            pe.wait_ge(const_in, 16)
            pe.wait_ge(par_step, EXP_STEPS + 43)
            for k in range(6):
                last = pe.transpose(ps[:, k, :], res[:, k, :], ident[0:Q, 0:Q])
            last.then_inc(turned, 1)

        @block.gpsimd
        def _(pool):
            pool.memset(zeros[:], 0.0).then_inc(cst, 1)
            with pool.Fori(0, B // 2) as i:
                for p in range(2):
                    pool.wait_ge(var_ready, 2 * i + p + 2)
                    pool.tensor_tensor(rstd[:, p], small[:, p, 4], minus_half[:], ALU.pow).then_inc(rstd_ready, 1)
            pool.wait_ge(par_ready, 1)
            with pool.Fori(0, G // 2) as i:
                for p in range(2):
                    pool.wait_ge(e_done, 2 * i + p + 1)
                    alpha = sh["modes"][:, 0, bass.ds((2 * i + p) * GQ, GQ)].unsqueeze(2).broadcast_to([P, GQ, T])
                    pool.tensor_tensor(earg[:, p], tcol.unsqueeze(1).broadcast_to([P, GQ, T]), alpha,
                                       ALU.mult).then_inc(earg_ready, 1)

        @block.vector
        def _(dve):
            steps = [0]

            def step(ins):
                steps[0] += 1
                ins.then_inc(par_step, 1)
                dve.wait_ge(par_step, steps[0])

            dve.sem_inc(x_free, 2)
            dve.memset(minus_half[:], -0.5).then_inc(var_ready, 1)
            dve.wait_ge(par_in, 80)
            tt, ts, stt = dve.tensor_tensor, dve.tensor_scalar, dve.scalar_tensor_tensor
            k_, r_, p_ = ex[:, 0], ex[:, 1], ex[:, 2]
            step(ts(logs[:], logs[:], -87.0, 88.0, ALU.max, ALU.min))
            step(ts(k_, logs[:], 1.4426950408889634, MAGIC, ALU.mult, ALU.add))
            step(ts(ex[:, 3], k_, MAGIC, None, ALU.subtract))
            step(stt(out=r_, in0=ex[:, 3], scalar=-LN2_HI, in1=logs[:], op0=ALU.mult, op1=ALU.add))
            step(stt(out=r_, in0=ex[:, 3], scalar=-LN2_LO, in1=r_, op0=ALU.mult, op1=ALU.add))
            step(ts(p_, r_, 1.0 / 5040, None, ALU.mult))
            for c in (1.0 / 720, 1.0 / 120, 1.0 / 24, 1.0 / 6, 0.5, 1.0):
                step(stt(out=p_, in0=p_, scalar=c, in1=r_, op0=ALU.add, op1=ALU.mult))
            step(ts(p_, p_, 1.0, None, ALU.add))
            step(ts(ex[:, 3].bitcast(I32), k_.bitcast(I32), 23, None, ALU.logical_shift_left))
            step(tt(ex[:, 4].bitcast(I32), p_.bitcast(I32), ex[:, 3].bitcast(I32), ALU.add))
            ea, aim, cre, cim = ex[:, 4, 0:P], par[:, 0, :], par[:, 1, :], par[:, 2, :]
            dtb = ex[:, 4, P:P + J].unsqueeze(2).broadcast_to([Q, J, N])

            def jn(ap):
                return ap.rearrange("q (j n) -> q j n", j=J)

            step(stt(out=jn(res[:, 0]), in0=jn(ea), scalar=-1.0, in1=dtb, op0=ALU.mult, op1=ALU.mult))
            step(tt(jn(w[:, 5]), jn(aim), dtb, ALU.mult))
            step(ts(w[:, 6], w[:, 5], INV_2PI, MAGIC, ALU.mult, ALU.add))
            step(ts(w[:, 7], w[:, 6], MAGIC, None, ALU.subtract))
            step(stt(out=w[:, 8], in0=w[:, 7], scalar=-PI_HI, in1=w[:, 5], op0=ALU.mult, op1=ALU.add))
            step(stt(out=w[:, 9], in0=w[:, 7], scalar=-PI_LO, in1=w[:, 8], op0=ALU.mult, op1=ALU.add))
            step(ts(w[:, 10], w[:, 9], 0.0, 2.0, ALU.is_ge, ALU.mult))
            step(ts(w[:, 10], w[:, 10], 1.0, None, ALU.subtract))
            step(tt(w[:, 11], w[:, 9], w[:, 10], ALU.mult))
            step(ts(w[:, 11], w[:, 11], 3.141592, None, ALU.min))
            sgn = w[:, 10]
            step(ts(res[:, 1], w[:, 11], INV_2PI, None, ALU.mult))
            step(tt(w[:, 12], aim, sgn, ALU.mult))
            step(tt(w[:, 13], cim, sgn, ALU.mult))
            dve.wait_ge(act_par, 4)
            e1, th, sn, hs, ai, ci = w[:, 1], w[:, 2], w[:, 3], w[:, 4], w[:, 12], w[:, 13]
            step(stt(out=w[:, 14], in0=e1, scalar=1.0, in1=th, op0=ALU.add, op1=ALU.mult))
            step(stt(out=w[:, 15], in0=hs, scalar=2.0, in1=hs, op0=ALU.mult, op1=ALU.mult))
            step(tt(w[:, 16], e1, w[:, 15], ALU.mult))
            step(tt(w[:, 17], w[:, 14], w[:, 16], ALU.subtract))
            step(tt(w[:, 18], e1, sn, ALU.mult))
            step(tt(w[:, 16], e1, w[:, 16], ALU.subtract))
            step(tt(w[:, 19], ea, ea, ALU.mult))
            step(tt(w[:, 20], ai, ai, ALU.mult))
            step(tt(w[:, 19], w[:, 19], w[:, 20], ALU.add))
            step(dve.reciprocal(w[:, 20], w[:, 19]))
            nr, ni = w[:, 17], w[:, 18]
            step(tt(w[:, 21], nr, ea, ALU.mult))
            step(tt(w[:, 22], ni, ai, ALU.mult))
            step(tt(w[:, 21], w[:, 22], w[:, 21], ALU.subtract))
            step(tt(w[:, 22], ni, ea, ALU.mult))
            step(tt(w[:, 23], nr, ai, ALU.mult))
            step(stt(out=w[:, 22], in0=w[:, 22], scalar=-1.0, in1=w[:, 23], op0=ALU.mult, op1=ALU.subtract))
            step(stt(out=w[:, 21], in0=w[:, 21], scalar=2.0 * K_SCALE, in1=w[:, 20], op0=ALU.mult, op1=ALU.mult))
            step(stt(out=w[:, 22], in0=w[:, 22], scalar=2.0 * K_SCALE, in1=w[:, 20], op0=ALU.mult, op1=ALU.mult))

            def cmul(outr, outi, ar, ai_, br, bi):
                dve_t = w[:, 23]
                step(tt(dve_t, ai_, bi, ALU.mult))
                step(tt(outr, ar, br, ALU.mult))
                step(tt(outr, outr, dve_t, ALU.subtract))
                step(tt(dve_t, ai_, br, ALU.mult))
                step(tt(outi, ar, bi, ALU.mult))
                step(tt(outi, outi, dve_t, ALU.add))

            cmul(res[:, 2], res[:, 3], cre, ci, w[:, 21], w[:, 22])
            cmul(res[:, 4], res[:, 5], res[:, 2], res[:, 3], w[:, 16], ni)
            dve.wait_ge(turned, 1)
            dve.tensor_copy(sh["modes"][:], ps[:]).then_inc(par_ready, 1)

            with dve.Fori(0, B // 2) as i:
                for p in range(2):
                    b = 2 * i + p
                    dve.wait_ge(x_in[p], 16 * i + 16)
                    for c in range(C):
                        last = dve.bn_stats(stats[:, p, c, :], xraw[:, p, c, :])
                    last.then_inc(stat_step, 1)
                    dve.wait_ge(stat_step, 7 * b + 1)
                    s = [stats[:, p, :, k] for k in range(6)]
                    tt(small[:, p, 0], s[1], s[4], ALU.add).then_inc(stat_step, 1)
                    tt(small[:, p, 1], s[1], s[4], ALU.subtract).then_inc(stat_step, 1)
                    tt(small[:, p, 2], s[2], s[5], ALU.add).then_inc(stat_step, 1)
                    dve.wait_ge(stat_step, 7 * b + 4)
                    ts(small[:, p, 5], small[:, p, 0], 0.5, None, ALU.mult).then_inc(stat_step, 1)
                    stt(out=small[:, p, 3], in0=small[:, p, 1], scalar=0.25, in1=small[:, p, 1],
                        op0=ALU.mult, op1=ALU.mult).then_inc(stat_step, 1)
                    ts(small[:, p, 2], small[:, p, 2], 1.0 / D, EPS, ALU.mult, ALU.add).then_inc(stat_step, 1)
                    dve.wait_ge(stat_step, 7 * b + 7)
                    tt(small[:, p, 4], small[:, p, 2], small[:, p, 3], ALU.add).then_inc(var_ready, 1)
                for p in range(2):
                    b = 2 * i + p
                    dve.wait_ge(rstd_ready, b + 1)
                    for c in range(C):
                        last = ts(sh["xn"][:, :, bass.ds(c * B + b, 1)].rearrange("p d o -> p (d o)"), xraw[:, p, c, :], small[:, p, 5, c:c + 1],
                                  rstd[:, p, c:c + 1], ALU.subtract, ALU.mult)
                    last.then_inc(x_free, 1)
            assert steps[0] == EXP_STEPS + 43, steps[0]


def mixer_groups(nc, io, sh):
    TERMS = ((0, 0), (1, 0), (0, 1))
    with ExitStack() as ctx:
        def sb(name, shape, dt=F32):
            return ctx.enter_context(nc.sbuf_tensor(name, shape, dt))

        def psum(name, shape, dt=F32):
            return ctx.enter_context(nc.psum_tensor(name, shape, dt))

        def sem(name):
            return ctx.enter_context(nc.semaphore(name))

        turns = sb("turns", [P, GQ, T])
        rounded = sb("rounded", [P, GQ, T])
        im = sb("im", [P, GQ, T])
        re = sb("re", [P, GQ, T])
        table = sb("table", [P, 2, 2, 2, GQ, P], F16)
        carry = sb("carry", [P, 2, 3, GQ, 1])
        tin = sb("tin", [P, GQ, 2, 2, P], F16)
        modes16 = sb("modes16", [P, 2, 2, Q], F16)
        weights = sb("weights", [P, 2, 4, GQ, GC], F16)
        id16 = sb("id16_b", [P, P], F16)
        ksb = sb("ksb", [GC, P, 2], F16)
        toep = sb("toep", [P, GC, P, 2], F16)
        xg = sb("xg", [P, 2, 2, GC, CB], F16)
        z = sb("z", [P, GQ, 2, SB])
        z16 = sb("z16", [P, 2, GQ, 2, SB], F16)
        za = sb("za", [P, GQ, 2, SB])
        zb = sb("zb", [P, GQ, 2, SB])
        dd = sb("dd", [P, GQ, 2])
        gl = sb("gl", [P, J, GQ, CB])
        half_pi = sb("half_pi", [P, 1])
        psY = psum("psY", [P, J, GQ, CB])
        psZ = psum("psZ", [P, 2, GQ // 2, 2, CB])
        psT = psum("psT", [P, 2, 2, 2, P], F16)
        psK = psum("psK", [P, 512])

        cst, id_ready, modes_hi, modes_lo, w_ready, x_hi, x_lo = (
            sem("cst_b"), sem("id_ready"), sem("modes_hi"), sem("modes_lo"), sem("w_ready"), sem("x_hi"), sem("x_lo"))
        frac_step, trig_step, table_step, carry_step, table_hi, re_lo, im_lo = (
            sem("frac_step"), sem("trig_step"), sem("table_step"), sem("carry_step"), sem("table_hi"),
            sem("re_lo"), sem("im_lo"))
        k_done, k_hi, k_lo, k_stored, toep_in, toep_used = (
            sem("k_done"), sem("k_hi"), sem("k_lo"), sem("k_stored"), sem("toep_in"), sem("toep_used"))
        turned, tin_ready, z_ready, z_step, rec_step, z_hi, z_lo, y_ready = (
            sem("turned_b"), sem("tin_ready"), sem("z_ready"), sem("z_step"), sem("rec_step"), sem("z_hi"),
            sem("z_lo"), sem("y_ready"))
        gelu_done, hi_done, lo_done = sem("gelu_done"), sem("hi_done"), sem("lo_done")

        tcol = sh["const"][:, C_POW:C_POW + T]
        mask = sh["const"][:, C_MASK:C_MASK + GQ * GC].rearrange("p (q m) -> p q m", q=GQ)
        y16 = sh["xn"][:].bitcast(F16).rearrange("p d (k c) -> p d k c", k=2)

        def mode(k, g):
            return sh["modes"][:, k, bass.ds(g * GQ, GQ)]

        def over(ap, *shape):
            for _ in shape:
                ap = ap.unsqueeze(len(ap.shape))
            return ap.broadcast_to([P, GQ, *shape])

        def there(g):
            return not isinstance(g, int) or 0 <= g < G

        def known(g, least):
            return not isinstance(g, int) or g >= least

        def rounds(eng, body):
            for g in range(-2, 2):
                body(g, g % 2)
            with eng.Fori(0, (G - 4) // 2) as i:
                body(2 * i + 2, 0)
                body(2 * i + 3, 1)
            for g in range(G - 2, G + 1):
                body(g, g % 2)

        block = ctx.enter_context(nc.Block())

        @block.sync
        def _(sp):
            for g in range(G):
                sp.wait_ge(k_lo, g + 1)
                sp.dma_start(io["kpad"][g * GC:(g + 1) * GC, 0:P], ksb[:]).then_inc(k_stored, 16)
                sp.wait_ge(k_stored, 16 * g + 16)
                if g > 0:
                    sp.wait_ge(toep_used, g)
                src = bass.AP(io["kpad"].tensor, g * (GC * 4 * P), [[2, P], [4 * P, GC], [1, 2 * P]])
                sp.dma_start(toep[:].rearrange("s d i k -> s d (i k)"), src).then_inc(toep_in, 16)

        @block.gpsimd
        def _(pool):
            def lower_re(g, p):
                pool.wait_ge(table_hi, 2 * g + 1)
                pool.tensor_tensor(table[:, p, 0, 1], re[:, :, 0:P], table[:, p, 0, 0], ALU.subtract).then_inc(re_lo, 1)

            def spread(g, p):
                if known(g, 2):
                    pool.wait_ge(k_done, g - 1)
                m = modes16[:, :, :, bass.ds(g * GQ, GQ)].rearrange("p k h q -> p (k h) q")
                pool.tensor_tensor(weights[:, p], mask.unsqueeze(1).broadcast_to([P, 4, GQ, GC]),
                                   m.unsqueeze(3).broadcast_to([P, 4, GQ, GC]), ALU.mult).then_inc(w_ready, 1)

            def lower_x(g, p):
                pool.wait_ge(x_hi, g + 1)
                pool.tensor_tensor(xg[:, p, 1], sh["xn"][:, bass.ds(g * GC, GC), :], xg[:, p, 0],
                                   ALU.subtract).then_inc(x_lo, 1)

            def lower_y(g):
                for j in range(J):
                    pool.wait_ge(hi_done, J * g + j + 1)
                    part = y16[:, bass.ds(g * GC, GC)].rearrange("p (q j) k c -> p j q k c", j=J)[:, j]
                    pool.tensor_tensor(part[:, :, 1], gl[:, j], part[:, :, 0], ALU.subtract).then_inc(lo_done, 1)

            def body(g, p):
                if there(g + 1):
                    lower_re(g + 1, 1 - p)
                if there(g + 2):
                    spread(g + 2, p)
                if there(g - 1):
                    lower_y(g - 1)
                if there(g + 2):
                    lower_x(g + 2, p)

            pool.memset(half_pi[:], PI / 2).then_inc(cst, 1)
            pool.wait_ge(modes_lo, 1)
            rounds(pool, body)

        @block.scalar
        def _(act):
            def gelu(g):
                for j in range(J):
                    act.wait_ge(y_ready, J * g + j + 1)
                    if known(g, 1):
                        act.wait_ge(lo_done, J * g - J + j + 1)
                    act.activation(gl[:, j], psY[:, j], ACT.Gelu, scale=1.0 / K_SCALE).then_inc(gelu_done, 1)

            def upper(g, p):
                for k, src in enumerate((re, im)):
                    act.wait_ge(table_step, 2 * g + 2)
                    if known(g, 2):
                        act.wait_ge(y_ready, J * g - J)
                    act.activation(table[:, p, k, 0], src[:, :, 0:P], ACT.Copy).then_inc(table_hi, 1)

            def upper_y(g, j):
                act.wait_ge(gelu_done, J * g + j + 1)
                dst = y16[:, bass.ds(g * GC, GC), 0, :].rearrange("p (q j) c -> p j q c", j=J)[:, j]
                act.activation(dst, gl[:, j], ACT.Copy).then_inc(hi_done, 1)

            def upper_x(g, p):
                if known(g, 2):
                    act.wait_ge(toep_used, g - 1)
                act.activation(xg[:, p, 0], sh["xn"][:, bass.ds(g * GC, GC), :], ACT.Copy).then_inc(x_hi, 1)

            def evacuate(g, i):
                act.wait_ge(turned, 4 * g + i + 1)
                act.activation(tin[:, 2 * i:2 * i + 2].rearrange("p q k h t -> p (q k h t)"),
                               psT[:].rearrange("p q k h t -> p (q k h t)"), ACT.Copy).then_inc(tin_ready, 1)

            def upper_k(g):
                act.wait_ge(k_done, g + 1)
                if known(g, 1):
                    act.wait_ge(k_stored, 16 * g)
                act.activation(ksb[:, :, 0], psK[0:GC, 0:P], ACT.Copy).then_inc(k_hi, 1)

            def trig(g):
                act.wait_ge(frac_step, 3 * g + 3)
                if known(g, 1):
                    act.wait_ge(re_lo, g)
                act.activation(re[:], im[:], ACT.Abs).then_inc(trig_step, 1)
                act.activation(im[:], im[:], ACT.Sin, scale=TWO_PI).then_inc(trig_step, 1)
                act.wait_ge(trig_step, 3 * g + 2)
                act.activation(re[:], re[:], ACT.Sin, scale=-TWO_PI, bias=half_pi[:]).then_inc(trig_step, 1)

            def body(g, p):
                if there(g - 1):
                    gelu(g - 1)
                if there(g + 1):
                    upper(g + 1, 1 - p)
                for i in range(4):
                    if there(g + 1):
                        evacuate(g + 1, i)
                    if there(g - 1):
                        upper_y(g - 1, i)
                    if i == 2 and there(g + 2):
                        upper_x(g + 2, p)
                if there(g + 1):
                    upper_k(g + 1)
                if there(g + 2):
                    trig(g + 2)

            act.wait_ge(cst, 1)
            rounds(act, body)

        @block.tensor
        def _(pe):
            def turn(g, p, i):
                if known(g, 1) or i > 0:
                    pe.wait_ge(tin_ready, 4 * g + i)
                for n in range(8):
                    q, k, part = n // 4, n // 2 % 2, n % 2
                    last = pe.transpose(psT[:, q, k, part], table[:, p, k, part, 2 * i + q], id16[:])
                last.then_inc(turned, 1)

            def kernel_values(g, p, i):
                if i == 0 and known(g, 1):
                    pe.wait_ge(k_lo, g)
                for q in range(2 * i, 2 * i + 2):
                    for k in range(2):
                        for wk, tk in TERMS:
                            last = pe.matmul(psK[0:GC, 0:P], weights[:, p, 2 * k + wk, q], table[:, p, k, tk, q],
                                             start=(q == 0 and k == 0 and wk + tk == 0),
                                             stop=(q == GQ - 1 and k == 1 and tk == 1), skip_group_check=True)
                if i == 3:
                    last.then_inc(k_done, 1)

            def states(g, p, i):
                pe.wait_ge(tin_ready, 4 * g + i + 1)
                if i % 2 == 0 and known(g, 1):
                    pe.wait_ge(z_step, 8 * g - 3 + 3 * (i // 2))
                for q in range(2 * i, 2 * i + 2):
                    for k in range(2):
                        for n, (tk, xk) in enumerate(TERMS):
                            for j in range(J):
                                last = pe.matmul(psZ[N * j:N * j + N, q // 4, q % 4, k, 0:SB],
                                                 tin[:, q, k, tk, N * j:N * j + N], xg[:, p, xk, J * q + j, 0:SB],
                                                 start=(n == 0), stop=(n == 2), skip_group_check=True)
                if i % 2 == 1:
                    last.then_inc(z_ready, 1)

            def within(g, p):
                pe.wait_ge(toep_in, 16 * g + 16)
                for j in range(J):
                    if known(g, 1):
                        pe.wait_ge(gelu_done, J * g - J + j + 1)
                    for q in range(GQ):
                        for n, (tk, xk) in enumerate(TERMS):
                            last = pe.matmul(psY[:, j, q], toep[:, J * q + j, :, tk], xg[:, p, xk, J * q + j],
                                             start=(q == 0 and n == 0), stop=False, skip_group_check=True)
                last.then_inc(toep_used, 1)

            def between(g, p):
                pe.wait_ge(z_lo, g + 1)
                for q in range(GQ):
                    for k in range(2):
                        for tk, zk in TERMS:
                            for j in range(J):
                                last = pe.matmul(psY[:, j, q, B:CB], table[N * j:N * j + N, p, k, tk, q],
                                                 z16[N * j:N * j + N, zk, q, k], start=False,
                                                 stop=(k == 1 and zk == 1), skip_group_check=True)
                                if q == GQ - 1 and k == 1 and zk == 1:
                                    last.then_inc(y_ready, 1)

            def body(g, p):
                if there(g):
                    within(g, p)
                if there(g + 1):
                    pe.wait_ge(re_lo, g + 2)
                    pe.wait_ge(im_lo, g + 2)
                    pe.wait_ge(w_ready, g + 2)
                    pe.wait_ge(x_lo, g + 2)
                    turn(g + 1, 1 - p, 0)
                    for i in range(4):
                        kernel_values(g + 1, 1 - p, i)
                        if i < 3:
                            turn(g + 1, 1 - p, i + 1)
                        states(g + 1, 1 - p, i)
                if there(g):
                    between(g, p)

            pe.wait_ge(id_ready, 1)
            rounds(pe, body)

        @block.vector
        def _(dve):
            tt, ts, stt = dve.tensor_tensor, dve.tensor_scalar, dve.scalar_tensor_tensor

            def phases(g):
                tt(turns[:], tcol.unsqueeze(1).broadcast_to([P, GQ, T]), over(mode(1, g), T),
                   ALU.mult).then_inc(frac_step, 1)
                dve.wait_ge(frac_step, 3 * g + 1)
                ts(rounded[:], turns[:], MAGIC, None, ALU.add).then_inc(frac_step, 1)

            def fractions(g):
                dve.wait_ge(frac_step, 3 * g + 2)
                if known(g, 1):
                    dve.wait_ge(im_lo, g)
                    dve.wait_ge(carry_step, 3 * g)
                stt(out=im[:], in0=rounded[:], scalar=MAGIC, in1=turns[:], op0=ALU.subtract,
                    op1=ALU.subtract).then_inc(frac_step, 1)

            def tables(g, p):
                dve.wait_ge(trig_step, 3 * g + 3)
                mag = sh["mag"][:, bass.ds(g * GQ, GQ), :]
                tt(re[:], re[:], mag, ALU.mult).then_inc(table_step, 1)
                tt(im[:], im[:], mag, ALU.mult).then_inc(table_step, 1)
                dve.wait_ge(table_step, 2 * g + 2)
                for k, (src, sign) in enumerate(((re, 1.0), (im, 1.0), (im, -1.0))):
                    ts(carry[:, p, k], src[:, :, P:P + 1], sign, None, ALU.mult).then_inc(carry_step, 1)

            def lower_im(g, p):
                dve.wait_ge(table_hi, 2 * g + 2)
                tt(table[:, p, 1, 1], im[:, :, 0:P], table[:, p, 1, 0], ALU.subtract).then_inc(im_lo, 1)

            def scaled(g):
                if known(g, 1):
                    dve.wait_ge(z_lo, g)
                ts(dd[:, :, 0:1], mode(4, g).unsqueeze(2), 1.0, None, ALU.mult).then_inc(z_step, 1)
                ts(dd[:, :, 1:2], mode(4, g).unsqueeze(2), -1.0, None, ALU.mult).then_inc(z_step, 1)
                dve.wait_ge(z_step, 8 * g + 2)
                half = GQ // 2
                for h in range(2):
                    rows = slice(h * half, h * half + half)
                    dve.wait_ge(z_ready, 2 * g + h + 1)
                    tt(za[:, rows], psZ[:, h, :, :, 0:SB], dd[:, rows].unsqueeze(3).broadcast_to([P, half, 2, SB]),
                       ALU.mult).then_inc(z_step, 1)
                    di = sh["modes"][:, 5, bass.ds(g * GQ + h * half, half)]
                    tt(zb[:, rows], psZ[:, h, :, ::-1, 0:SB],
                       di.unsqueeze(2).unsqueeze(3).broadcast_to([P, half, 2, SB]), ALU.mult).then_inc(z_step, 1)
                    dve.wait_ge(z_step, 8 * g + 4 + 3 * h)
                    tt(z[:, rows], za[:, rows], zb[:, rows], ALU.add).then_inc(z_step, 1)

            def recurrence(g, p):
                dve.wait_ge(z_step, 8 * g + 8)
                dve.wait_ge(carry_step, 3 * g + 3)
                zc = z[:].rearrange("p q k (c b) -> p q k c b", b=B)
                a4 = za[:].rearrange("p q k (c b) -> p q k c b", b=B)
                b4 = zb[:].rearrange("p q k (c b) -> p q k c b", b=B)
                by_re = carry[:, p, 0].unsqueeze(3).broadcast_to([P, GQ, 2, B])
                by_im = carry[:, p, 1:3].rearrange("p k q o -> p q k o").broadcast_to([P, GQ, 2, B])
                n = 24 * g
                for c in range(1, C - 1):
                    tt(a4[:, :, :, c], zc[:, :, :, c - 1], by_re, ALU.mult).then_inc(rec_step, 1)
                    tt(b4[:, :, :, c], zc[:, :, ::-1, c - 1], by_im, ALU.mult).then_inc(rec_step, 1)
                    dve.wait_ge(rec_step, n + 4 * c - 2)
                    tt(a4[:, :, :, c], a4[:, :, :, c], b4[:, :, :, c], ALU.add).then_inc(rec_step, 1)
                    dve.wait_ge(rec_step, n + 4 * c - 1)
                    tt(zc[:, :, :, c], zc[:, :, :, c], a4[:, :, :, c], ALU.add).then_inc(rec_step, 1)
                    dve.wait_ge(rec_step, n + 4 * c)
                if known(g, 1):
                    dve.wait_ge(y_ready, J * g)
                ts(z16[:, 0], z[:], 1.0, None, ALU.mult).then_inc(z_hi, 1)
                dve.wait_ge(z_hi, g + 1)
                tt(z16[:, 1], z[:], z16[:, 0], ALU.subtract).then_inc(z_lo, 1)

            def lower_k(g):
                dve.wait_ge(k_hi, g + 1)
                tt(ksb[:, :, 1], psK[0:GC, 0:P], ksb[:, :, 0], ALU.subtract).then_inc(k_lo, 1)

            def body(g, p):
                if there(g + 2):
                    phases(g + 2)
                if there(g + 1):
                    lower_im(g + 1, 1 - p)
                if there(g + 2):
                    fractions(g + 2)
                if there(g):
                    recurrence(g, p)
                if there(g + 1):
                    lower_k(g + 1)
                    scaled(g + 1)
                if there(g + 2):
                    tables(g + 2, p)

            ts(modes16[:, :, 0], sh["modes"][:, 2:4], 1.0, None, ALU.mult).then_inc(modes_hi, 1)
            dve.wait_ge(modes_hi, 1)
            tt(modes16[:, :, 1], sh["modes"][:, 2:4], modes16[:, :, 0], ALU.subtract).then_inc(modes_lo, 1)
            ts(id16[:], sh["const"][:, C_ID:C_ID + P], 1.0, None, ALU.mult).then_inc(id_ready, 1)
            rounds(dve, body)


def feed_forward(nc, io, sh):
    S = B * L // (ST * P)
    PAIRS = ST // 2
    LN_STEPS = 10
    TERMS = ((0, 0), (0, 1), (1, 0))
    with ExitStack() as ctx:
        def sb(name, shape, dt=F32):
            return ctx.enter_context(nc.sbuf_tensor(name, shape, dt))

        def psum(name, shape, dt=F32):
            return ctx.enter_context(nc.psum_tensor(name, shape, dt))

        def sem(name):
            return ctx.enter_context(nc.semaphore(name))

        wp_raw = sb("wp_raw", [P, KD, D])
        wp = sb("wp", [P, 2, KD, D], F16)
        w1_raw = sb("w1_raw", [P, KD, F])
        w2_raw = sb("w2_raw", [P, KF, D])
        w1 = sb("w1", [P, 2, 2, KD, F], F16)
        w2 = sb("w2", [P, 2, 2, KF, D], F16)
        bias = sb("bias", [P, D])
        b1_raw = sb("b1_raw", [E * KF, P])
        b1 = sb("b1", [P, E * KF])
        b1_now = sb("b1_now", [P, 2, KF])
        b2 = sb("b2", [P, E, D])
        id16 = sb("id16", [P, P], F16)
        rev16 = sb("rev16", [P, P], F16)
        xres = sb("xres", [P, 4, ST, D])
        yT = sb("yT", [P, 2, KD, 2, P], F16)
        z = sb("zproj", [P, ST, D])
        hin = sb("hin", [P, ST, D])
        hin16 = sb("hin16", [P, 2, ST, D], F16)
        hT = sb("hT", [P, 2, 2, KD, ST, P], F16)
        a32 = sb("a32", [P, 2, ST * P])
        a16 = sb("a16", [P, 2, KF, ST * P], F16)
        ff = sb("ff", [P, 2, ST, D])
        NA, NX, NB = range(3)
        stats = sb("stats_c", [P, 3, ST, 6])
        small = sb("small_c", [P, 3, 4, ST])
        var = sb("var", [P, 3, ST])
        rstd = sb("rstd_c", [P, 3, ST])
        nmr = sb("nmr", [P, 3, ST])
        minus_half = sb("minus_half_c", [P, ST])
        ps_yT = psum("ps_yT", [P, 2, KD, 2, P])
        ps_z = psum("ps_z", [P, 2, D])
        ps_hT = psum("ps_hT", [P, 2, KD, 2, P], F16)
        A_BANKS = 3
        ps_a = psum("ps_a", [P, A_BANKS, ST * P])
        ps_f1 = psum("ps_f1", [P, 2, D])
        ps_f = [ps_a[:, 2].rearrange("p (t d) -> p t d", t=2), ps_f1]

        start_in, w1_in, w2_in, x_in, stored = (
            sem("start_in"), sem("w1_in"), sem("w2_in"), [sem(f"x_in_c{k}") for k in range(4)],
            [sem("stored0"), sem("stored1")])
        cst, b1_ready, id_done, turned_w, wp_hi, wp_lo, w1_hi, w1_lo, w2_hi, w2_lo = (
            sem("cst_c"), sem("b1_ready"), sem("id_done"), sem("turned_w"), sem("wp_hi"), sem("wp_lo"), sem("w1_hi"), sem("w1_lo"), sem("w2_hi"),
            sem("w2_lo"))
        yT_ready, yT_done, z_ready, hT_ready, hT_done = (
            sem("yT_ready"), sem("yT_done"), sem("z_ready_c"), sem("hT_ready"), sem("hT_done"))
        a_ready, a_hi, a_lo, f_ready = sem("a_ready"), sem("a_hi"), sem("a_lo"), sem("f_ready")
        ln_step, ln_var, ln_rstd, ln_nmr, ln_done = (
            [sem(f"{n}{k}") for k in range(3)] for n in ("ln_step", "ln_var", "ln_rstd", "ln_nmr", "ln_done"))
        x1_done, hin_hi, hin_lo, out_ready = sem("x1_done"), sem("hin_hi"), sem("hin_lo"), sem("out_ready")
        y16 = sh["xn"][:].bitcast(F16).rearrange("p d (k c) -> p d k c", k=2)
        ident = sh["const"][:, C_ID:C_ID + P]

        def windows(body):
            def run(eng):
                body(0, 0)
                with eng.Fori(0, (S - 4) // 4) as i:
                    for k in range(4):
                        body(4 * i + k + 1, (k + 1) % 4)
                for s in range(S - 3, S):
                    body(s, s % 4)
            return run

        def known(s, least):
            return not isinstance(s, int) or s >= least

        def there(s):
            return not isinstance(s, int) or s < S

        def expert(s, k, ahead=0):
            if isinstance(s, int):
                return (s + ahead) // 2
            return (s - k) // 2 + (k + ahead) // 2

        block = ctx.enter_context(nc.Block())

        @block.sync
        def _(sp):
            def load_w1(e):
                sp.dma_start(w1_raw[:], io["w1"][bass.ds(e, 1)].rearrange("o (k p) f -> p (o k) f", p=P)).then_inc(w1_in, 16)

            def load_w2(e):
                sp.dma_start(w2_raw[:], io["w2"][bass.ds(e, 1)].rearrange("o (k p) d -> p (o k) d", p=P)).then_inc(w2_in, 16)

            def load_x(s, k):
                sp.dma_start(xres[:, k], io["x"].rearrange("b (u t p) d -> (b u) p t d", p=P, t=ST)[bass.ds(s, 1)]
                             .rearrange("o p t d -> p (o t) d")).then_inc(x_in[k], 16)

            def store(s, k):
                sp.wait_ge(out_ready, s + 1)
                sp.dma_start(io["out"].rearrange("b (u t p) d -> (b u) p t d", p=P, t=ST)[bass.ds(s, 1)]
                             .rearrange("o p t d -> p (o t) d"), ff[:, k % 2]).then_inc(stored[k % 2], 16)

            sp.dma_start(wp_raw[:], io["W"].rearrange("(k p) d -> p k d", p=P)).then_inc(start_in, 16)
            sp.dma_start(b1_raw[:], io["b1"].rearrange("e (k p) -> (e k) p", p=P)).then_inc(start_in, 16)
            sp.dma_start(bias[:], io["b"].partition_broadcast(P)).then_inc(start_in, 16)
            for e in range(E):
                sp.dma_start(b2[:, e], io["b2"][e].partition_broadcast(P)).then_inc(start_in, 16)
            load_x(0, 0)
            load_w1(0)
            load_w2(0)
            load_x(1, 1)
            load_x(2, 2)
            sp.wait_ge(w1_lo, 1)
            load_w1(1)

            def body(s, k):
                if known(s, 1):
                    store(s - 1, k - 1)
                if there(s + 3):
                    load_x(s + 3, (k + 3) % 4)
                e = expert(s, k)
                if k % 2 == 0 and (not isinstance(s, int) or e + 1 < E):
                    sp.wait_ge(w2_lo, e + 1)
                    load_w2(e + 1)
                if k % 2 == 1 and (not isinstance(s, int) or e + 2 < E):
                    sp.wait_ge(w1_lo, e + 2)
                    load_w1(e + 2)

            windows(body)(sp)
            store(S - 1, (S - 1) % 4)
            for p in range(2):
                sp.wait_ge(stored[p], 16 * (S // 2))

        @block.gpsimd
        def _(pool):
            pool.memset(minus_half[:], -0.5).then_inc(cst, 1)
            pool.wait_ge(cst, 1)

            def power(n, s):
                pool.wait_ge(ln_var[n], s + 1)
                pool.tensor_tensor(rstd[:, n], var[:, n], minus_half[:], ALU.pow).then_inc(ln_rstd[n], 1)
                pool.wait_ge(ln_rstd[n], s + 1)
                pool.tensor_tensor(nmr[:, n], small[:, n, 0], rstd[:, n], ALU.mult).then_inc(ln_nmr[n], 1)

            def residual(s, k):
                for t in range(ST):
                    last = pool.tensor_scalar(z[:, t], z[:, t], small[:, NA, 0, t:t + 1], rstd[:, NA, t:t + 1],
                                              ALU.add, ALU.mult)
                last.then_inc(ln_done[NA], 1)
                pool.wait_ge(ln_done[NA], s + 1)
                pool.wait_ge(x_in[k], 16 * (s // 4) + 16 if isinstance(s, int) else 4 * (s - k) + 16)
                pool.tensor_tensor(xres[:, k], xres[:, k], z[:], ALU.add).then_inc(x1_done, 1)

            def finish(s, k):
                pool.wait_ge(ln_done[NB], s + 1)
                pool.tensor_tensor(ff[:, k % 2], ff[:, k % 2], xres[:, k], ALU.add).then_inc(out_ready, 1)

            def body(s, k):
                if there(s + 1):
                    power(NA, s + 1)
                    residual(s + 1, (k + 1) % 4)
                if known(s, 1):
                    power(NB, s - 1)
                if there(s + 1):
                    power(NX, s + 1)
                if known(s, 1):
                    finish(s - 1, (k - 1) % 4)

            power(NA, 0)
            residual(0, 0)
            power(NX, 0)
            windows(body)(pool)
            power(NB, S - 1)
            finish(S - 1, (S - 1) % 4)

        @block.scalar
        def _(act):
            def evacuate_yT(s, t):
                act.wait_ge(yT_ready, ST * s + t + 1)
                if known(s, 1) or t >= 2:
                    act.wait_ge(z_ready, PAIRS * s + t // 2)
                act.activation(yT[:, t % 2], ps_yT[:, t % 2], ACT.Copy).then_inc(yT_done, 1)

            def normalise(n, s, out, data):
                act.wait_ge(ln_nmr[n], s + 1)
                for t in range(ST):
                    last = act.activation(out[:, t], data[:, t], ACT.Identity, scale=rstd[:, n, t:t + 1],
                                          bias=nmr[:, n, t:t + 1])
                last.then_inc(ln_done[n], 1)

            def hidden(s, k, f):
                act.wait_ge(a_ready, KF * s + f + 1)
                if k % 2 == 0 and f == 0:
                    act.wait_ge(b1_ready, expert(s, k) + 1)
                b = b1_now[:, k // 2, f:f + 1]
                act.activation(a16[:, 0, f], ps_a[:, f % A_BANKS], ACT.Gelu_apprx_tanh, scale=1.0 / W_SCALE, bias=b)
                if known(s, 1) or f >= 2:
                    act.wait_ge(a_lo, KF * s + f - 1)
                act.activation(a32[:, f % 2], ps_a[:, f % A_BANKS], ACT.Gelu_apprx_tanh, scale=1.0 / W_SCALE,
                               bias=b).then_inc(a_hi, 1)

            def split_w1(e, ep):
                act.wait_ge(w1_in, 16 * e + 16)
                act.activation(w1[:, ep, 0], w1_raw[:], ACT.Copy, scale=W_SCALE).then_inc(w1_hi, 1)

            def split_w2(e, ep):
                act.wait_ge(w2_in, 16 * e + 16)
                act.activation(w2[:, ep, 0], w2_raw[:], ACT.Copy, scale=W_SCALE).then_inc(w2_hi, 1)

            def body(s, k):
                for f in range(KF):
                    hidden(s, k, f)
                if there(s + 2):
                    evacuate_yT(s + 2, 0)
                    evacuate_yT(s + 2, 1)
                if known(s, 1):
                    normalise(NB, s - 1, ff[:, (k - 1) % 2], ff[:, (k - 1) % 2])
                if there(s + 1):
                    normalise(NX, s + 1, hin, xres[:, (k + 1) % 4])
                if there(s + 2):
                    evacuate_yT(s + 2, 2)
                    evacuate_yT(s + 2, 3)
                e = expert(s, k)
                if k % 2 == 0 and (not isinstance(s, int) or e + 1 < E):
                    split_w1(e + 1, (k // 2 + 1) % 2)
                if k % 2 == 1 and (not isinstance(s, int) or e + 1 < E):
                    split_w2(e + 1, (k // 2 + 1) % 2)

            act.wait_ge(turned_w, 1)
            act.activation(wp[:, 0], ps_a[:, 0].rearrange("p (k e) -> p k e", k=KD), ACT.Copy, scale=W_SCALE)\
                .then_inc(wp_hi, 1)
            for t in range(ST):
                evacuate_yT(0, t)
            split_w1(0, 0)
            split_w2(0, 0)
            normalise(NX, 0, hin, xres[:, 0])
            for t in range(ST):
                evacuate_yT(1, t)
            windows(body)(act)
            normalise(NB, S - 1, ff[:, (S - 1) % 2], ff[:, (S - 1) % 2])

        @block.tensor
        def _(pe):
            def turn_y(s, k, t):
                if known(s, 1) or t >= 2:
                    pe.wait_ge(yT_done, ST * s + t - 1)
                e = expert(s, k)
                c = (k % 2) * ST + t
                for h in range(KD):
                    for part in range(2):
                        tile = y16[:, h * P:(h + 1) * P, part, bass.ds(c * B + e, 1)].rearrange("p d o -> p (d o)")
                        last = pe.matmul(ps_yT[:, t % 2, h, part], tile, rev16[:], start=True, stop=True)
                last.then_inc(yT_ready, 1)

            def project(s, r):
                if known(s, 1) or r == 1:
                    pe.wait_ge(ln_step[NA], LN_STEPS * s + 1 if r == 1 else LN_STEPS * s - LN_STEPS + 3)
                for t in range(2):
                    pe.wait_ge(yT_done, ST * s + 2 * r + t + 1)
                    n = 0
                    for wk, yk in TERMS:
                        for h in range(KD):
                            last = pe.matmul(ps_z[:, t], yT[:, t, h, yk], wp[:, wk, h], start=(n == 0), stop=(n == 5))
                            n += 1
                last.then_inc(z_ready, 1)

            def turn_h(s, r):
                pe.wait_ge(hin_lo, s + 1)
                if known(s, 1) or r == 1:
                    pe.wait_ge(hT_done, PAIRS * s + r)
                for t in range(2):
                    for h in range(KD):
                        for part in range(2):
                            last = pe.transpose(ps_hT[:, t, h, part], hin16[:, part, 2 * r + t, h * P:(h + 1) * P], id16[:])
                last.then_inc(hT_ready, 1)

            def layer1(s, k, f):
                ep = k // 2
                if f >= A_BANKS:
                    pe.wait_ge(a_hi, KF * s + f - A_BANKS + 1)
                elif known(s, 1):
                    pe.wait_ge(a_hi, KF * s)
                    if f == 2:
                        pe.wait_ge(ln_step[NB], LN_STEPS * s - LN_STEPS + 1)
                n = 0
                for wk, xk in TERMS:
                    for h in range(KD):
                        last = pe.matmul(ps_a[:, f % A_BANKS], w1[:, ep, wk, h, f * P:(f + 1) * P],
                                         hT[:, k % 2, xk, h].rearrange("p t n -> p (t n)"), start=(n == 0), stop=(n == 5))
                        n += 1
                last.then_inc(a_ready, 1)

            def layer2(s, k, t):
                ep = k // 2
                if t == 0:
                    pe.wait_ge(a_hi, KF * s + 6)
                if t == 2 and known(s, 1):
                    pe.wait_ge(ln_step[NB], LN_STEPS * s - LN_STEPS + 3)
                for f in range(KF):
                    if t == 0:
                        pe.wait_ge(a_lo, KF * s + f + 1)
                    for n, (wk, ak) in enumerate(TERMS):
                        last = pe.matmul(ps_f[t // 2][:, t % 2], a16[:, ak, f, t * P:(t + 1) * P], w2[:, ep, wk, f],
                                         start=(f == 0 and n == 0), stop=(f == KF - 1 and n == 2))
                if t % 2 == 1:
                    last.then_inc(f_ready, 1)

            def body(s, k):
                pe.wait_ge(hT_done, PAIRS * s + PAIRS)
                if k % 2 == 0:
                    pe.wait_ge(w1_lo, expert(s, k) + 1)
                for f in range(KF):
                    layer1(s, k, f)
                nxt, nk, far, fk = s + 1, (k + 1) % 4, s + 2, (k + 2) % 4
                if there(far):
                    turn_y(far, fk, 0)
                    turn_y(far, fk, 1)
                if k % 2 == 0:
                    pe.wait_ge(w2_lo, expert(s, k) + 1)
                layer2(s, k, 0)
                layer2(s, k, 1)
                if there(far):
                    project(far, 0)
                    turn_y(far, fk, 2)
                    turn_y(far, fk, 3)
                layer2(s, k, 2)
                if there(nxt):
                    turn_h(nxt, 0)
                layer2(s, k, 3)
                if there(nxt):
                    turn_h(nxt, 1)
                if there(far):
                    project(far, 1)

            pe.wait_ge(start_in, 16 * (3 + E))
            for h in range(KD):
                for k in range(KD):
                    last = pe.transpose(ps_a[:, 0, h * D + k * P:h * D + (k + 1) * P], wp_raw[:, k, h * P:(h + 1) * P], ident)
            last = pe.transpose(ps_a[:, 1, 0:E * KF], b1_raw[:], ident[0:E * KF, 0:E * KF])
            last.then_inc(turned_w, 1)
            pe.wait_ge(id_done, 2)
            turn_y(0, 0, 0)
            turn_y(0, 0, 1)
            pe.wait_ge(wp_lo, 2)
            project(0, 0)
            turn_y(0, 0, 2)
            turn_y(0, 0, 3)
            project(0, 1)
            turn_y(1, 1, 0)
            turn_y(1, 1, 1)
            turn_h(0, 0)
            project(1, 0)
            turn_y(1, 1, 2)
            turn_y(1, 1, 3)
            turn_h(0, 1)
            project(1, 1)
            windows(body)(pe)

        @block.vector
        def _(dve):
            tt, ts, stt = dve.tensor_tensor, dve.tensor_scalar, dve.scalar_tensor_tensor

            def biased(n, s, r, out, data, scale, b):
                stt(out=out[:, 2 * r:2 * r + 2], in0=data, scalar=scale, in1=b.unsqueeze(1).broadcast_to([P, 2, D]),
                    op0=ALU.mult, op1=ALU.add).then_inc(ln_step[n], 1)
                dve.wait_ge(ln_step[n], LN_STEPS * s + 2 * r + 1)
                for t in range(2 * r, 2 * r + 2):
                    last = dve.bn_stats(stats[:, n, t], out[:, t])
                last.then_inc(ln_step[n], 1)

            def variance(n, s):
                st = [stats[:, n, :, k] for k in range(6)]
                sm = [small[:, n, k] for k in range(4)]
                if known(s, 1):
                    dve.wait_ge(ln_nmr[n], s)
                dve.wait_ge(ln_step[n], LN_STEPS * s + 4)
                tt(sm[0], st[1], st[4], ALU.add).then_inc(ln_step[n], 1)
                tt(sm[1], st[1], st[4], ALU.subtract).then_inc(ln_step[n], 1)
                tt(sm[2], st[2], st[5], ALU.add).then_inc(ln_step[n], 1)
                dve.wait_ge(ln_step[n], LN_STEPS * s + 7)
                stt(out=sm[3], in0=sm[1], scalar=0.25, in1=sm[1], op0=ALU.mult, op1=ALU.mult).then_inc(ln_step[n], 1)
                ts(sm[2], sm[2], 1.0 / D, EPS, ALU.mult, ALU.add).then_inc(ln_step[n], 1)
                ts(sm[0], sm[0], -0.5, None, ALU.mult).then_inc(ln_step[n], 1)
                dve.wait_ge(ln_step[n], LN_STEPS * s + 10)
                tt(var[:, n], sm[2], sm[3], ALU.add).then_inc(ln_var[n], 1)

            def z_pair(s, r):
                dve.wait_ge(z_ready, PAIRS * s + r + 1)
                if r == 0 and known(s, 1):
                    dve.wait_ge(x1_done, s)
                biased(NA, s, r, z, ps_z[:], 1.0 / W_SCALE, bias[:])

            def f_pair(s, k, r):
                dve.wait_ge(f_ready, PAIRS * s + r + 1)
                if r == 0 and known(s, 2):
                    dve.wait_ge(stored[k % 2], stored_count(s, k))
                e = expert(s, k)
                biased(NB, s, r, ff[:, k % 2], ps_f[r][:], 1.0 / W_SCALE, b2[:, bass.ds(e, 1)].rearrange("p o d -> p (o d)"))

            def stored_count(s, k):
                return 16 * (s // 2) if isinstance(s, int) else 8 * (s - k % 2)

            def x1_statistics(s, k):
                dve.wait_ge(x1_done, s + 1)
                for t in range(ST):
                    last = dve.bn_stats(stats[:, NX, t], xres[:, k, t])
                last.then_inc(ln_step[NX], 4)
                variance(NX, s)

            def split_h(s):
                dve.wait_ge(ln_done[NX], s + 1)
                if known(s, 1):
                    dve.wait_ge(hT_ready, PAIRS * s)
                ts(hin16[:, 0], hin[:], 1.0, None, ALU.mult).then_inc(hin_hi, 1)
                dve.wait_ge(hin_hi, s + 1)
                tt(hin16[:, 1], hin[:], hin16[:, 0], ALU.subtract).then_inc(hin_lo, 1)

            def evacuate_h(s, k, r):
                dve.wait_ge(hT_ready, PAIRS * s + r + 1)
                for h in range(KD):
                    last = dve.tensor_copy(
                        hT[:, k % 2, :, h, 2 * r:2 * r + 2], ps_hT[:, :, h].rearrange("p t k n -> p k t n"))
                last.then_inc(hT_done, 1)

            def lower(s, f):
                dve.wait_ge(a_hi, KF * s + f + 1)
                tt(a16[:, 1, f], a32[:, f % 2], a16[:, 0, f], ALU.subtract).then_inc(a_lo, 1)

            def split_w(e, ep, w, raw, hi, lo):
                dve.wait_ge(hi, e + 1)
                stt(out=w[:, ep, 1], in0=raw[:], scalar=W_SCALE, in1=w[:, ep, 0], op0=ALU.mult,
                    op1=ALU.subtract).then_inc(lo, 1)

            def next_b1(e, ep):
                ts(b1_now[:, ep], b1[:, bass.ds(e * KF, KF)], 1.0, None, ALU.mult).then_inc(b1_ready, 1)

            def body(s, k):
                nxt, nk, far, fk = s + 1, (k + 1) % 4, s + 2, (k + 2) % 4
                lower(s, 0)
                if there(nxt):
                    z_pair(nxt, 1)
                lower(s, 1)
                if there(nxt):
                    variance(NA, nxt)
                lower(s, 2)
                if known(s, 1):
                    f_pair(s - 1, (k - 1) % 4, 1)
                lower(s, 3)
                if known(s, 1):
                    variance(NB, s - 1)
                for f in range(4, KF):
                    lower(s, f)
                if there(nxt):
                    x1_statistics(nxt, nk)
                if there(nxt):
                    split_h(nxt)
                if there(far):
                    z_pair(far, 0)
                f_pair(s, k, 0)
                if there(nxt):
                    evacuate_h(nxt, nk, 0)
                    evacuate_h(nxt, nk, 1)
                e = expert(s, k)
                if k % 2 == 0 and (not isinstance(s, int) or e + 1 < E):
                    split_w(e + 1, (k // 2 + 1) % 2, w1, w1_raw, w1_hi, w1_lo)
                if k % 2 == 1 and (not isinstance(s, int) or e + 1 < E):
                    split_w(e + 1, (k // 2 + 1) % 2, w2, w2_raw, w2_hi, w2_lo)
                    next_b1(e + 1, (k // 2 + 1) % 2)

            ts(id16[:], ident, 1.0, None, ALU.mult).then_inc(id_done, 1)
            ts(rev16[:], sh["const"][:, C_REV:C_REV + P], 1.0, None, ALU.mult).then_inc(id_done, 1)
            dve.wait_ge(turned_w, 1)
            dve.tensor_copy(b1[:], ps_a[:, 1, 0:E * KF]).then_inc(wp_lo, 1)
            dve.wait_ge(wp_hi, 1)
            stt(out=wp[:, 1], in0=ps_a[:, 0].rearrange("p (k e) -> p k e", k=KD), scalar=W_SCALE, in1=wp[:, 0],
                op0=ALU.mult, op1=ALU.subtract).then_inc(wp_lo, 1)
            z_pair(0, 0)
            z_pair(0, 1)
            variance(NA, 0)
            dve.wait_ge(wp_lo, 2)
            next_b1(0, 0)
            split_w(0, 0, w1, w1_raw, w1_hi, w1_lo)
            split_w(0, 0, w2, w2_raw, w2_hi, w2_lo)
            x1_statistics(0, 0)
            split_h(0)
            evacuate_h(0, 0, 0)
            z_pair(1, 0)
            evacuate_h(0, 0, 1)
            windows(body)(dve)
            f_pair(S - 1, (S - 1) % 4, 1)
            variance(NB, S - 1)


def sandwich(nc, io):
    with ExitStack() as ctx:
        sh = {"const": ctx.enter_context(nc.sbuf_tensor("constants", [P, C_END], F32)),
              "xn": ctx.enter_context(nc.sbuf_tensor("xn", [P, D, CB], F32))}
        with ExitStack() as mixer:
            sh["mag"] = mixer.enter_context(nc.sbuf_tensor("magnitudes", [P, Q, T], F32))
            sh["modes"] = mixer.enter_context(nc.sbuf_tensor("modes", [P, 6, Q], F32))
            mixer_prologue(nc, io, sh)
            mixer_groups(nc, io, sh)
        feed_forward(nc, io, sh)


_INS = ["L0_attn_x", "L0_attn_log_dt", "L0_attn_log_A_real", "L0_attn_A_imag", "L0_attn_C_real", "L0_attn_C_imag",
        "L0_attn_W", "L0_attn_b", "L0_ffn_w1", "L0_ffn_b1", "L0_ffn_w2", "L0_ffn_b2"]


def kernel(**inputs):
    import numpy as _np
    import concourse.bacc as _bacc
    from concourse import mybir as _mybir
    from concourse.bass_utils import run_bass_kernel_spmd as _run

    nc = _bacc.Bacc("TRN2", target_bir_lowering=False, num_devices=1)
    arrays, io = {}, {}
    for name in _INS:
        a = _np.ascontiguousarray(inputs[name])
        arrays[f"in_{name}_dram"] = a
        io[name.split("_", 2)[2]] = nc.dram_tensor(
            f"in_{name}_dram", a.shape, _mybir.dt.from_np(a.dtype), kind="ExternalInput").ap()
    const = _np.zeros((P, C_END), _np.float32)
    const[:, C_ID:C_ID + P] = _np.eye(P)
    const[:, C_REV:C_REV + P] = _np.eye(P)[::-1]
    const[:, C_POW:C_POW + P] = _np.arange(P)[::-1]
    const[:, C_POW + P] = P
    mask = const[:, C_MASK:].reshape(P, GQ, GC)
    for q in range(GQ):
        for j in range(J):
            mask[j * N:(j + 1) * N, q, J * q + j] = 1.0
    arrays["in_const_dram"] = const
    io["const"] = nc.dram_tensor("in_const_dram", const.shape, _mybir.dt.float32, kind="ExternalInput").ap()
    io["kpad"] = nc.dram_tensor("kpad", [D, 2 * P, 2], _mybir.dt.float16, kind="Internal").ap()
    io["out"] = nc.dram_tensor("out_0_dram", [B, L, D], _mybir.dt.float32, kind="ExternalOutput").ap()
    sandwich(nc, io)
    r = _run(nc, [arrays], core_ids=[0])
    return r.results[0]["out_0_dram"]
```

```python
from contextlib import ExitStack

import concourse.bass as bass
from concourse import mybir

F32 = mybir.dt.float32
F16 = mybir.dt.float16
I32 = mybir.dt.int32
ALU = mybir.AluOpType
ACT = mybir.ActivationFunctionType

P = 128
B, L, D = 8, 1024, 256
N = 32
E, F = 8, 1024
C = L // P
CB = C * B
SB = (C - 1) * B
J = P // N
Q = D // J
T = P + 1
GQ = 8
GC = GQ * J
G = Q // GQ
KD = D // P
KF = F // P
ST = 4
EPS = 1e-5
PI = 3.14159265358979
TWO_PI = 6.283185
INV_2PI = 0.15915494309189535
PI_HI, PI_LO = 6.28125, 0.0019353071795864769
LN2_HI, LN2_LO = 0.693359375, -2.12194440054690583e-4
EXP_STEPS = 15
MAGIC = 12582912.0
K_SCALE, W_SCALE = 64.0, 64.0
C_ID, C_REV, C_POW, C_MASK = 0, P, 2 * P, 2 * P + T
C_END = C_MASK + GQ * GC


def of_group(sh, k, g):
    return sh["modes"][:, k, bass.ds(g * GQ, GQ)]


def turn_counts(pool, sh, g):
    tcol = sh["const"][:, C_POW:C_POW + T]
    pool.tensor_tensor(sh["turns"][:], tcol.unsqueeze(1).broadcast_to([P, GQ, T]),
                       of_group(sh, 1, g).unsqueeze(2).broadcast_to([P, GQ, T]), ALU.mult).then_inc(sh["turns_done"], 1)


def phases(dve, sh, g):
    turns, im, frac_step = sh["turns"], sh["im"], sh["frac_step"]
    dve.wait_ge(sh["turns_done"], g + 1)
    dve.tensor_scalar(im[:], turns[:], MAGIC, None, ALU.add).then_inc(frac_step, 1)
    dve.wait_ge(frac_step, 2 * g + 1)
    dve.scalar_tensor_tensor(out=im[:], in0=im[:], scalar=MAGIC, in1=turns[:], op0=ALU.subtract,
                             op1=ALU.subtract).then_inc(frac_step, 1)


def trigonometry(act, sh, g):
    re, im, trig_step = sh["re"], sh["im"], sh["trig_step"]
    act.wait_ge(sh["frac_step"], 2 * g + 2)
    act.activation(re[:], im[:], ACT.Abs).then_inc(trig_step, 1)
    act.wait_ge(trig_step, 3 * g + 1)
    act.activation(re[:], re[:], ACT.Sin, scale=-TWO_PI, bias=sh["half_pi"][:]).then_inc(trig_step, 1)
    act.activation(im[:], im[:], ACT.Sin, scale=TWO_PI).then_inc(trig_step, 1)


def mixer_prologue(nc, io, sh):
    with ExitStack() as ctx:
        def sb(name, shape, dt=F32):
            return ctx.enter_context(nc.sbuf_tensor(name, shape, dt))

        def sem(name):
            return ctx.enter_context(nc.semaphore(name))

        par = sb("par", [Q, 3, P])
        logs = sb("logs", [Q, P + J])
        ex = sb("ex", [Q, 5, P + J])
        w = sb("w", [Q, 24, P])
        res = sb("res", [Q, 6, P])
        xraw = sb("xraw", [P, B - 1, C, D])
        stats = sb("stats", [P, B, C, 6])
        small = sb("small", [P, 5, B, C])
        neg_mean = sb("neg_mean", [P, B, C])
        minus_half = sb("minus_half", [P, 2, C])
        rstd = sb("rstd", [P, B, C])
        nmr = sb("nmr_x", [P, B, C])
        zeros = sb("zeros", [P, KD, P, 2], F16)
        wp_raw = sb("wp_raw", [P, KD, D])
        b1_raw = sb("b1_raw", [E * KF, P])
        ps = ctx.enter_context(nc.psum_tensor("psP", [P, 512], F32))
        psW = ctx.enter_context(nc.psum_tensor("psW", [P, KD, D], F32))
        psB = ctx.enter_context(nc.psum_tensor("psB", [P, 512], F32))

        par_in, x_in, const_in = sem("par_in"), [sem(f"x_in{b}") for b in range(B)], sem("const_in")
        stat_done, var_step, var_ready, rstd_ready, nmr_ready = (
            sem("stat_done"), sem("var_step"), sem("var_ready"), sem("rstd_ready"), sem("nmr_ready"))
        par_step, act_par, turned, par_ready = sem("par_step"), sem("act_par"), sem("turned"), sem("par_ready")
        cst, dve_args, pool_args, pad_done = sem("cst"), sem("dve_args"), sem("pool_args"), sem("pad_done")
        w_in, bias_in, w_turned, w_hi = sem("w_in"), sem("bias_in"), sem("w_turned"), sem("w_hi")
        x_free, half_pi_set = sem("x_free"), sem("half_pi_set")

        ident = sh["const"][:, C_ID:C_ID + P]
        tcol = sh["const"][:, C_POW:C_POW + T]
        ACT_ROWS, POOL_ROWS, DVE_ROWS = (0, 2, 4), (1, 3, 5), (6, 7)

        def exponents(eng, q, done):
            qs = slice(q * Q // 4, (q + 1) * Q // 4)
            alpha = sh["modes"][:, 0, qs].unsqueeze(2).broadcast_to([P, Q // 4, T])
            eng.tensor_tensor(sh["mag"][:, qs], tcol.unsqueeze(1).broadcast_to([P, Q // 4, T]), alpha,
                              ALU.mult).then_inc(done, 1)

        def normalise(eng, b):
            eng.wait_ge(rstd_ready, b // 2 + 1)
            for c in range(C):
                eng.tensor_scalar(sh["xn"][:, :, c * B + b], xraw[:, b % (B - 1), c], neg_mean[:, b, c:c + 1],
                                  rstd[:, b, c:c + 1], ALU.add, ALU.mult)

        block = ctx.enter_context(nc.Block())

        @block.sync
        def _(sp):
            sp.dma_start(logs[:, 0:P], io["log_A_real"].rearrange("(q j) n -> q (j n)", j=J)).then_inc(par_in, 16)
            for k, name in enumerate(("A_imag", "C_real", "C_imag")):
                sp.dma_start(par[:, k, :], io[name].rearrange("(q j) n -> q (j n)", j=J)).then_inc(par_in, 16)
            sp.dma_start(logs[:, P:P + J], io["log_dt"].rearrange("(q j) -> q j", j=J)).then_inc(par_in, 16)
            sp.dma_start(sh["const"][:], io["const"]).then_inc(const_in, 16)
            for b in range(B):
                if b == B - 1:
                    sp.wait_ge(x_free, 1)
                sp.dma_start(xraw[:, b % (B - 1)], io["x"][b].rearrange("(c p) d -> p c d", p=P)).then_inc(x_in[b], 16)
            sp.dma_start(wp_raw[:], io["W"].rearrange("(k p) d -> p k d", p=P)).then_inc(w_in, 16)
            sp.dma_start(b1_raw[:], io["b1"].rearrange("e (k p) -> (e k) p", p=P)).then_inc(w_in, 16)
            sp.dma_start(sh["bias"][:], io["b"].partition_broadcast(P)).then_inc(bias_in, 16)
            sp.wait_ge(bias_in, 16)
            sp.wait_ge(cst, 1)
            sp.dma_start(io["kpad"].rearrange("(h p) t k -> p h (t k)", p=P)[:, :, 2 * P:4 * P],
                         zeros[:].rearrange("p h t k -> p h (t k)")).then_inc(pad_done, 16)
            sp.wait_ge(pad_done, 16)

        @block.scalar
        def _(act):
            act.wait_ge(par_step, EXP_STEPS + 1)
            act.activation(w[:, 1], res[:, 0], ACT.Exp).then_inc(act_par, 1)
            act.activation(w[:, 2], res[:, 0], ACT.Tanh, scale=0.5).then_inc(act_par, 1)
            act.wait_ge(par_step, EXP_STEPS + 10)
            act.activation(w[:, 3], w[:, 11], ACT.Sin).then_inc(act_par, 1)
            act.activation(w[:, 4], w[:, 11], ACT.Sin, scale=0.5).then_inc(act_par, 1)
            for b in ACT_ROWS:
                act.wait_ge(nmr_ready, b // 2 + 1)
                for c in range(C):
                    last = act.activation(sh["xn"][:, :, c * B + b], xraw[:, b % (B - 1), c], ACT.Identity,
                                   scale=rstd[:, b, c:c + 1], bias=nmr[:, b, c:c + 1])
                last.then_inc(x_free, 1)
            act.wait_ge(w_turned, 1)
            act.activation(sh["wp"][:, 0], psW[:], ACT.Copy, scale=W_SCALE).then_inc(w_hi, 1)
            for q in range(4):
                if q < 3:
                    act.wait_ge(dve_args, q + 1)
                else:
                    act.wait_ge(pool_args, 1)
                mag = sh["mag"][:, q * Q // 4:(q + 1) * Q // 4]
                act.activation(mag, mag, ACT.Exp)
            act.wait_ge(half_pi_set, 1)
            trigonometry(act, sh, 0)

        @block.tensor
        def _(pe):
            pe.wait_ge(const_in, 16)
            pe.wait_ge(w_in, 32)
            for h in range(KD):
                for k in range(KD):
                    last = pe.transpose(psW[:, h, k * P:(k + 1) * P], wp_raw[:, k, h * P:(h + 1) * P], ident)
            last = pe.transpose(psB[:, 0:E * KF], b1_raw[:], ident[0:E * KF, 0:E * KF])
            last.then_inc(w_turned, 1)
            pe.wait_ge(par_step, EXP_STEPS + 43)
            for k in range(6):
                last = pe.transpose(ps[:, k * Q:(k + 1) * Q], res[:, k, :], ident[0:Q, 0:Q])
            last.then_inc(turned, 1)

        @block.gpsimd
        def _(pool):
            pool.memset(sh["half_pi"][:], PI / 2).then_inc(half_pi_set, 1)
            pool.memset(zeros[:], 0.0).then_inc(cst, 1)
            pool.memset(minus_half[:], -0.5).then_inc(cst, 1)
            for r in range(B // 2):
                pair = slice(2 * r, 2 * r + 2)
                if r == 0:
                    pool.wait_ge(cst, 2)
                pool.wait_ge(var_ready, r + 1)
                pool.tensor_tensor(rstd[:, pair], small[:, 4, pair], minus_half[:], ALU.pow).then_inc(rstd_ready, 1)
                pool.wait_ge(rstd_ready, r + 1)
                pool.tensor_tensor(nmr[:, pair], neg_mean[:, pair], rstd[:, pair], ALU.mult).then_inc(nmr_ready, 1)
                if 2 * r + 1 in POOL_ROWS:
                    normalise(pool, 2 * r + 1)
            pool.wait_ge(par_ready, 1)
            turn_counts(pool, sh, 0)
            exponents(pool, 3, pool_args)

        @block.vector
        def _(dve):
            tt, ts, stt = dve.tensor_tensor, dve.tensor_scalar, dve.scalar_tensor_tensor
            steps = [0]
            HEAD = 4

            def statistics(tile):
                b, c = tile // C, tile % C
                if c == 0:
                    dve.wait_ge(x_in[b], 16)
                dve.bn_stats(stats[:, b, c], xraw[:, b % (B - 1), c]).then_inc(stat_done, 1)
                if tile % (2 * C) == 2 * C - 1:
                    variance(b // 2)

            def variance(r):
                pair = slice(2 * r, 2 * r + 2)
                st = [stats[:, pair, :, k] for k in range(6)]
                sm = [small[:, k, pair] for k in range(5)]
                dve.wait_ge(stat_done, 2 * C * (r + 1))
                tt(sm[0], st[1], st[4], ALU.add).then_inc(var_step, 1)
                tt(sm[1], st[1], st[4], ALU.subtract).then_inc(var_step, 1)
                tt(sm[2], st[2], st[5], ALU.add).then_inc(var_step, 1)
                dve.wait_ge(var_step, 6 * r + 3)
                ts(neg_mean[:, pair], sm[0], -0.5, None, ALU.mult).then_inc(var_step, 1)
                stt(out=sm[3], in0=sm[1], scalar=0.25, in1=sm[1], op0=ALU.mult, op1=ALU.mult).then_inc(var_step, 1)
                ts(sm[2], sm[2], 1.0 / D, EPS, ALU.mult, ALU.add).then_inc(var_step, 1)
                dve.wait_ge(var_step, 6 * r + 6)
                tt(sm[4], sm[2], sm[3], ALU.add).then_inc(var_ready, 1)

            def step(ins):
                steps[0] += 1
                ins.then_inc(par_step, 1)
                if steps[0] > HEAD:
                    statistics(steps[0] - HEAD - 1)
                dve.wait_ge(par_step, steps[0])

            dve.wait_ge(par_in, 80)
            k_, r_, p_ = ex[:, 0], ex[:, 1], ex[:, 2]
            step(ts(logs[:], logs[:], -87.0, 88.0, ALU.max, ALU.min))
            step(ts(k_, logs[:], 1.4426950408889634, MAGIC, ALU.mult, ALU.add))
            step(ts(ex[:, 3], k_, MAGIC, None, ALU.subtract))
            step(stt(out=r_, in0=ex[:, 3], scalar=-LN2_HI, in1=logs[:], op0=ALU.mult, op1=ALU.add))
            step(stt(out=r_, in0=ex[:, 3], scalar=-LN2_LO, in1=r_, op0=ALU.mult, op1=ALU.add))
            step(ts(p_, r_, 1.0 / 5040, None, ALU.mult))
            for c in (1.0 / 720, 1.0 / 120, 1.0 / 24, 1.0 / 6, 0.5, 1.0):
                step(stt(out=p_, in0=p_, scalar=c, in1=r_, op0=ALU.add, op1=ALU.mult))
            step(ts(p_, p_, 1.0, None, ALU.add))
            step(ts(ex[:, 3].bitcast(I32), k_.bitcast(I32), 23, None, ALU.logical_shift_left))
            step(tt(ex[:, 4].bitcast(I32), p_.bitcast(I32), ex[:, 3].bitcast(I32), ALU.add))
            ea, aim, cre, cim = ex[:, 4, 0:P], par[:, 0, :], par[:, 1, :], par[:, 2, :]
            dtb = ex[:, 4, P:P + J].unsqueeze(2).broadcast_to([Q, J, N])

            def jn(ap):
                return ap.rearrange("q (j n) -> q j n", j=J)

            step(stt(out=jn(res[:, 0]), in0=jn(ea), scalar=-1.0, in1=dtb, op0=ALU.mult, op1=ALU.mult))
            step(tt(jn(w[:, 5]), jn(aim), dtb, ALU.mult))
            step(ts(w[:, 6], w[:, 5], INV_2PI, MAGIC, ALU.mult, ALU.add))
            step(ts(w[:, 7], w[:, 6], MAGIC, None, ALU.subtract))
            step(stt(out=w[:, 8], in0=w[:, 7], scalar=-PI_HI, in1=w[:, 5], op0=ALU.mult, op1=ALU.add))
            step(stt(out=w[:, 9], in0=w[:, 7], scalar=-PI_LO, in1=w[:, 8], op0=ALU.mult, op1=ALU.add))
            step(ts(w[:, 10], w[:, 9], 0.0, 2.0, ALU.is_ge, ALU.mult))
            step(ts(w[:, 10], w[:, 10], 1.0, None, ALU.subtract))
            step(tt(w[:, 11], w[:, 9], w[:, 10], ALU.mult))
            step(ts(w[:, 11], w[:, 11], 3.141592, None, ALU.min))
            sgn = w[:, 10]
            step(ts(res[:, 1], w[:, 11], INV_2PI, None, ALU.mult))
            step(tt(w[:, 12], aim, sgn, ALU.mult))
            step(tt(w[:, 13], cim, sgn, ALU.mult))
            dve.wait_ge(act_par, 4)
            e1, th, sn, hs, ai, ci = w[:, 1], w[:, 2], w[:, 3], w[:, 4], w[:, 12], w[:, 13]
            step(stt(out=w[:, 14], in0=e1, scalar=1.0, in1=th, op0=ALU.add, op1=ALU.mult))
            step(stt(out=w[:, 15], in0=hs, scalar=2.0, in1=hs, op0=ALU.mult, op1=ALU.mult))
            step(tt(w[:, 16], e1, w[:, 15], ALU.mult))
            step(tt(w[:, 17], w[:, 14], w[:, 16], ALU.subtract))
            step(tt(w[:, 18], e1, sn, ALU.mult))
            step(tt(w[:, 16], e1, w[:, 16], ALU.subtract))
            step(tt(w[:, 19], ea, ea, ALU.mult))
            step(tt(w[:, 20], ai, ai, ALU.mult))
            step(tt(w[:, 19], w[:, 19], w[:, 20], ALU.add))
            step(dve.reciprocal(w[:, 20], w[:, 19]))
            nr, ni = w[:, 17], w[:, 18]
            step(tt(w[:, 21], nr, ea, ALU.mult))
            step(tt(w[:, 22], ni, ai, ALU.mult))
            step(tt(w[:, 21], w[:, 22], w[:, 21], ALU.subtract))
            step(tt(w[:, 22], ni, ea, ALU.mult))
            step(tt(w[:, 23], nr, ai, ALU.mult))
            step(stt(out=w[:, 22], in0=w[:, 22], scalar=-1.0, in1=w[:, 23], op0=ALU.mult, op1=ALU.subtract))
            step(stt(out=w[:, 21], in0=w[:, 21], scalar=2.0 * K_SCALE, in1=w[:, 20], op0=ALU.mult, op1=ALU.mult))
            step(stt(out=w[:, 22], in0=w[:, 22], scalar=2.0 * K_SCALE, in1=w[:, 20], op0=ALU.mult, op1=ALU.mult))

            def cmul(outr, outi, ar, ai_, br, bi):
                dve_t = w[:, 23]
                step(tt(dve_t, ai_, bi, ALU.mult))
                step(tt(outr, ar, br, ALU.mult))
                step(tt(outr, outr, dve_t, ALU.subtract))
                step(tt(dve_t, ai_, br, ALU.mult))
                step(tt(outi, ar, bi, ALU.mult))
                step(tt(outi, outi, dve_t, ALU.add))

            cmul(res[:, 2], res[:, 3], cre, ci, w[:, 21], w[:, 22])
            cmul(res[:, 4], res[:, 5], res[:, 2], res[:, 3], w[:, 16], ni)
            assert steps[0] == EXP_STEPS + 43, steps[0]
            for tile in range(steps[0] - HEAD, B * C):
                statistics(tile)
            dve.wait_ge(turned, 1)
            dve.tensor_copy(sh["modes"][:], ps[:, 0:6 * Q].rearrange("p (k q) -> p k q", k=6)).then_inc(par_ready, 1)
            dve.wait_ge(par_ready, 1)
            dve.wait_ge(const_in, 16)
            for q in range(3):
                exponents(dve, q, dve_args)
            phases(dve, sh, 0)
            for b in DVE_ROWS:
                normalise(dve, b)
            ts(sh["id16"][:], ident, 1.0, None, ALU.mult)
            ts(sh["rev16"][:], sh["const"][:, C_REV:C_REV + P], 1.0, None, ALU.mult)
            dve.wait_ge(w_turned, 1)
            dve.tensor_copy(sh["b1"][:], psB[:, 0:E * KF])
            dve.wait_ge(w_hi, 1)
            stt(out=sh["wp"][:, 1], in0=psW[:], scalar=W_SCALE, in1=sh["wp"][:, 0], op0=ALU.mult,
                op1=ALU.subtract)


def mixer_groups(nc, io, sh):
    TERMS = ((0, 0), (0, 1), (1, 0))
    BANKS, BC = GQ // 2, GC // (GQ // 2)
    with ExitStack() as ctx:
        def sb(name, shape, dt=F32):
            return ctx.enter_context(nc.sbuf_tensor(name, shape, dt))

        def psum(name, shape, dt=F32):
            return ctx.enter_context(nc.psum_tensor(name, shape, dt))

        def sem(name):
            return ctx.enter_context(nc.semaphore(name))

        table = sb("table", [P, 2, 2, 2, GQ, P], F16)
        carry = sb("carry", [P, 2, 3, GQ, 1])
        tin = sb("tin", [P, 2, 2, 2, 2, P], F16)
        modes16 = sb("modes16", [P, 2, 2, Q], F16)
        weights = sb("weights", [P, 2, 4, GQ, GC], F16)
        ksb = sb("ksb", [GC, P, 2], F16)
        toep = sb("toep", [P, GC, P, 2], F16)
        xg = sb("xg", [P, 2, 2, GC, CB], F16)
        z = sb("z", [P, GQ, 2, SB])
        zdiag = sb("zdiag", [P, 2, GQ, 2, J, SB], F16)
        za = sb("za", [P, GQ, 2, SB])
        zb = sb("zb", [P, GQ, 2, SB])
        z16 = za[:].rearrange("p q k c -> p (q k c)").bitcast(F16).rearrange("p (h q k c) -> p h q k c", h=2, q=GQ, k=2)
        dd = sb("dd", [P, Q, 2])
        gl = sb("gl", [P, BANKS, BC, CB])
        warm = sb("warm", [P, 2])
        psY = psum("psY", [P, BANKS, BC, CB])
        psZ = psum("psZ", [P, 2, GQ // 2, 2, CB])
        psT = psum("psT", [P, 2, 2, 2, P], F16)
        psK = psum("psK", [P, 512])

        cst, dd_ready, zeroed, modes_hi, modes_lo, w_ready, x_hi, x_lo = (
            sem("cst_b"), sem("dd_ready"), sem("zeroed"), sem("modes_hi"), sem("modes_lo"),
            sem("w_ready"), sem("x_hi"), sem("x_lo"))
        re_done, im_done, carry_step, table_hi, re_lo, im_lo = (
            sem("re_done"), sem("im_done"), sem("carry_step"), sem("table_hi"), sem("re_lo"), sem("im_lo"))
        re, im, frac_step, trig_step = (sh[k] for k in ("re", "im", "frac_step", "trig_step"))
        k_done, k_hi, k_lo, k_stored, toep_in, toep_used = (
            sem("k_done"), sem("k_hi"), sem("k_lo"), sem("k_stored"), sem("toep_in"), sem("toep_used"))
        turned, tin_ready, z_ready, z_step, rec_step, z_hi, z_lo, z_spread, y_ready = (
            sem("turned_b"), sem("tin_ready"), sem("z_ready"), sem("z_step"), sem("rec_step"), sem("z_hi"),
            sem("z_lo"), sem("z_spread"), sem("y_ready"))
        gelu_done, hi_done, lo_done = sem("gelu_done"), sem("hi_done"), sem("lo_done")

        mask = sh["const"][:, C_MASK:C_MASK + GQ * GC].rearrange("p (q m) -> p q m", q=GQ)
        y16 = sh["xn"][:].bitcast(F16).rearrange("p d (k c) -> p d k c", k=2)

        def there(g):
            return not isinstance(g, int) or 0 <= g < G

        def known(g, least):
            return not isinstance(g, int) or g >= least

        def rounds(eng, body):
            for g in range(-2, 2):
                body(g, g % 2)
            with eng.Fori(0, (G - 4) // 2) as i:
                body(2 * i + 2, 0)
                body(2 * i + 3, 1)
            for g in range(G - 2, G + 1):
                body(g, g % 2)

        block = ctx.enter_context(nc.Block())

        @block.sync
        def _(sp):
            for g in range(G):
                sp.wait_ge(k_lo, g + 1)
                sp.dma_start(io["kpad"][g * GC:(g + 1) * GC, 0:P], ksb[:]).then_inc(k_stored, 16)
                sp.wait_ge(k_stored, 16 * g + 16)
                if g > 0:
                    sp.wait_ge(toep_used, g)
                src = bass.AP(io["kpad"].tensor, g * (GC * 4 * P), [[2, P], [4 * P, GC], [1, 2 * P]])
                sp.dma_start(toep[:].rearrange("s d i k -> s d (i k)"), src).then_inc(toep_in, 16)

        @block.gpsimd
        def _(pool):
            def lower_re(g, p):
                pool.wait_ge(table_hi, 2 * g + 1)
                pool.tensor_tensor(table[:, p, 0, 1], re[:, :, 0:P], table[:, p, 0, 0], ALU.subtract).then_inc(re_lo, 1)

            def times_magnitude(g):
                pool.wait_ge(trig_step, 3 * g + 2)
                pool.tensor_tensor(re[:], re[:], sh["mag"][:, bass.ds(g * GQ, GQ), :], ALU.mult).then_inc(re_done, 1)

            def spread(g, p):
                if known(g, 2):
                    pool.wait_ge(k_done, g - 1)
                if isinstance(g, int) and g == 0:
                    pool.wait_ge(modes_lo, 1)
                m = modes16[:, :, :, bass.ds(g * GQ, GQ)].rearrange("p k h q -> p (k h) q")
                pool.tensor_tensor(weights[:, p], mask.unsqueeze(1).broadcast_to([P, 4, GQ, GC]),
                                   m.unsqueeze(3).broadcast_to([P, 4, GQ, GC]), ALU.mult).then_inc(w_ready, 1)

            def lower_x(g, p):
                pool.wait_ge(x_hi, g + 1)
                pool.tensor_tensor(xg[:, p, 1], sh["xn"][:, bass.ds(g * GC, GC), :], xg[:, p, 0],
                                   ALU.subtract).then_inc(x_lo, 1)

            def lower_y(g):
                for i in range(BANKS // 2 if isinstance(g, int) and g == G - 1 else BANKS):
                    pool.wait_ge(hi_done, BANKS * g + i + 1)
                    part = y16[:, bass.ds(g * GC + i * BC, BC)]
                    pool.tensor_tensor(part[:, :, 1], gl[:, i], part[:, :, 0], ALU.subtract).then_inc(lo_done, 1)

            def body(g, p):
                if not known(g, -1):
                    times_magnitude(0)
                    spread(0, 0)
                    return
                if there(g + 1):
                    lower_re(g + 1, 1 - p)
                if isinstance(g, int) and g == -1:
                    lower_x(0, 0)
                if there(g + 2):
                    pool.wait_ge(frac_step, 2 * g + 4)
                    turn_counts(pool, sh, g + 2)
                    lower_x(g + 2, p)
                if there(g - 1):
                    lower_y(g - 1)
                if there(g + 2):
                    spread(g + 2, p)
                    times_magnitude(g + 2)

            pool.memset(warm[:], 0.0).then_inc(cst, 1)
            rounds(pool, body)

        @block.scalar
        def _(act):
            def gelu(g, banks):
                for i in banks:
                    act.wait_ge(y_ready, BANKS * g + i + 1)
                    if known(g, 1):
                        act.wait_ge(lo_done, BANKS * g - BANKS + i + 1)
                    act.activation(gl[:, i], psY[:, i], ACT.Gelu, scale=1.0 / K_SCALE).then_inc(gelu_done, 1)

            def upper(g, p):
                for k in range(2):
                    act.wait_ge((re_done, im_done)[k], g + 1)
                    if known(g, 2):
                        act.wait_ge(y_ready, BANKS * g - BANKS)
                    act.activation(table[:, p, k, 0], (re, im)[k][:, :, 0:P], ACT.Copy).then_inc(table_hi, 1)

            def upper_y(g, i):
                act.wait_ge(gelu_done, BANKS * g + i + 1)
                act.activation(y16[:, bass.ds(g * GC + i * BC, BC), 0, :], gl[:, i], ACT.Copy).then_inc(hi_done, 1)

            def upper_x(g, p):
                if known(g, 2):
                    act.wait_ge(toep_used, g - 1)
                act.activation(xg[:, p, 0], sh["xn"][:, bass.ds(g * GC, GC), :], ACT.Copy).then_inc(x_hi, 1)

            def evacuate(g, i):
                act.wait_ge(turned, 4 * g + i + 1)
                act.activation(tin[:, i % 2].rearrange("p q k h t -> p (q k h t)"),
                               psT[:].rearrange("p q k h t -> p (q k h t)"), ACT.Copy).then_inc(tin_ready, 1)

            def upper_k(g):
                act.wait_ge(k_done, g + 1)
                if known(g, 1):
                    act.wait_ge(k_stored, 16 * g)
                act.activation(ksb[:, :, 0], psK[0:GC, 0:P], ACT.Copy).then_inc(k_hi, 1)

            def body(g, p):
                if there(g - 1):
                    act.activation(warm[:, 1:2], warm[:, 0:1], ACT.Gelu)
                    gelu(g - 1, range(BANKS - 1))
                if there(g + 1):
                    upper(g + 1, 1 - p)
                if there(g - 1):
                    gelu(g - 1, (BANKS - 1,))
                if there(g + 2):
                    upper_x(g + 2, p)
                for i in range(4):
                    if there(g + 1):
                        evacuate(g + 1, i)
                    if i == 0 and there(g + 1):
                        upper_k(g + 1)
                    if there(g - 1):
                        upper_y(g - 1, i)
                if there(g + 2) and known(g, -1):
                    act.wait_ge(re_lo, g + 2)
                    trigonometry(act, sh, g + 2)

            act.wait_ge(cst, 1)
            rounds(act, body)

        @block.tensor
        def _(pe):
            def turn(g, p, i):
                if known(g, 1) or i > 0:
                    pe.wait_ge(tin_ready, 4 * g + i)
                for n in range(8):
                    q, k, part = n // 4, n // 2 % 2, n % 2
                    last = pe.transpose(psT[:, q, k, part], table[:, p, k, part, 2 * i + q], sh["id16"][:])
                last.then_inc(turned, 1)

            def kernel_values(g, p):
                if known(g, 1):
                    pe.wait_ge(k_lo, g)
                for q in range(GQ):
                    for k in range(2):
                        for wk, tk in TERMS:
                            last = pe.matmul(psK[0:GC, 0:P], weights[:, p, 2 * k + wk, q], table[:, p, k, tk, q],
                                             start=(q == 0 and k == 0 and wk + tk == 0),
                                             stop=(q == GQ - 1 and k == 1 and wk == 1), skip_group_check=True)
                last.then_inc(k_done, 1)

            def states(g, p, i):
                pe.wait_ge(tin_ready, 4 * g + i + 1)
                if i == 0:
                    pe.wait_ge(x_lo, g + 1)
                if i % 2 == 0 and known(g, 1):
                    pe.wait_ge(z_step, 6 * g - 4 + 3 * (i // 2))
                for q in range(2 * i, 2 * i + 2):
                    for k in range(2):
                        for n, (tk, xk) in enumerate(TERMS):
                            for j in range(J):
                                last = pe.matmul(psZ[N * j:N * j + N, q // 4, q % 4, k, 0:SB],
                                                 tin[:, i % 2, q % 2, k, tk, N * j:N * j + N], xg[:, p, xk, J * q + j, 0:SB],
                                                 start=(n == 0), stop=(n == 2), skip_group_check=True)
                if i % 2 == 1:
                    last.then_inc(z_ready, 1)

            def within(g, p):
                pe.wait_ge(toep_in, 16 * g + 16)
                for i in range(BANKS):
                    if known(g, 1):
                        pe.wait_ge(gelu_done, BANKS * g - BANKS + i + 1)
                    for c in range(BC):
                        for n, (tk, xk) in enumerate(TERMS):
                            last = pe.matmul(psY[:, i, c], toep[:, BC * i + c, :, tk], xg[:, p, xk, BC * i + c],
                                             start=(c == 0 and n == 0), stop=False, skip_group_check=True)
                last.then_inc(toep_used, 1)

            def between(g, p):
                pe.wait_ge(z_spread, J * g + J)
                for q in range(GQ):
                    c = q % 2 * J
                    for k in range(2):
                        for tk, zk in TERMS:
                            last = pe.matmul(psY[:, q // 2, c:c + J, B:CB], table[:, p, k, tk, q],
                                             zdiag[:, zk, q, k].rearrange("p j c -> p (j c)"), start=False,
                                             stop=(q % 2 == 1 and k == 1 and tk == 1), skip_group_check=True)
                    if q % 2 == 1:
                        last.then_inc(y_ready, 1)

            def body(g, p):
                if there(g):
                    within(g, p)
                if there(g + 1):
                    pe.wait_ge(re_lo, g + 2)
                    pe.wait_ge(im_lo, g + 2)
                    pe.wait_ge(w_ready, g + 2)
                    turn(g + 1, 1 - p, 0)
                    kernel_values(g + 1, 1 - p)
                    for i in range(4):
                        if i < 3:
                            turn(g + 1, 1 - p, i + 1)
                        states(g + 1, 1 - p, i)
                if there(g):
                    between(g, p)

            rounds(pe, body)

        @block.vector
        def _(dve):
            tt, ts, stt = dve.tensor_tensor, dve.tensor_scalar, dve.scalar_tensor_tensor

            def tables(g, p):
                dve.wait_ge(trig_step, 3 * g + 3)
                tt(im[:], im[:], sh["mag"][:, bass.ds(g * GQ, GQ), :], ALU.mult).then_inc(im_done, 1)
                dve.wait_ge(im_done, g + 1)
                for k, sign in ((1, 1.0), (2, -1.0)):
                    ts(carry[:, p, k], im[:, :, P:P + 1], sign, None, ALU.mult).then_inc(carry_step, 1)
                dve.wait_ge(re_done, g + 1)
                ts(carry[:, p, 0], re[:, :, P:P + 1], 1.0, None, ALU.mult).then_inc(carry_step, 1)

            def lower_im(g, p):
                dve.wait_ge(table_hi, 2 * g + 2)
                tt(table[:, p, 1, 1], im[:, :, 0:P], table[:, p, 1, 0], ALU.subtract).then_inc(im_lo, 1)

            def scaled(g):
                if known(g, 1):
                    dve.wait_ge(z_spread, J * g)
                half = GQ // 2
                for h in range(2):
                    rows = slice(h * half, h * half + half)
                    dve.wait_ge(z_ready, 2 * g + h + 1)
                    dr = dd[:, bass.ds(g * GQ + h * half, half)]
                    tt(za[:, rows], psZ[:, h, :, :, 0:SB], dr.unsqueeze(3).broadcast_to([P, half, 2, SB]),
                       ALU.mult).then_inc(z_step, 1)
                    di = sh["modes"][:, 5, bass.ds(g * GQ + h * half, half)]
                    tt(zb[:, rows], psZ[:, h, :, ::-1, 0:SB],
                       di.unsqueeze(2).unsqueeze(3).broadcast_to([P, half, 2, SB]), ALU.mult).then_inc(z_step, 1)
                    dve.wait_ge(z_step, 6 * g + 2 + 3 * h)
                    tt(z[:, rows], za[:, rows], zb[:, rows], ALU.add).then_inc(z_step, 1)

            def recurrence(g, p, chunks):
                if 1 in chunks:
                    dve.wait_ge(z_step, 6 * g + 6)
                    dve.wait_ge(carry_step, 3 * g + 3)
                zc = z[:].rearrange("p q k (c b) -> p q k c b", b=B)
                a4 = za[:].rearrange("p q k (c b) -> p q k c b", b=B)
                b4 = zb[:].rearrange("p q k (c b) -> p q k c b", b=B)
                by_re = carry[:, p, 0].unsqueeze(3).broadcast_to([P, GQ, 2, B])
                by_im = carry[:, p, 1:3].rearrange("p k q o -> p q k o").broadcast_to([P, GQ, 2, B])
                n = 24 * g
                for c in chunks:
                    tt(a4[:, :, :, c], zc[:, :, :, c - 1], by_re, ALU.mult).then_inc(rec_step, 1)
                    tt(b4[:, :, :, c], zc[:, :, ::-1, c - 1], by_im, ALU.mult).then_inc(rec_step, 1)
                    dve.wait_ge(rec_step, n + 4 * c - 3)
                    tt(zc[:, :, :, c], zc[:, :, :, c], a4[:, :, :, c], ALU.add).then_inc(rec_step, 1)
                    dve.wait_ge(rec_step, n + 4 * c - 1)
                    tt(zc[:, :, :, c], zc[:, :, :, c], b4[:, :, :, c], ALU.add).then_inc(rec_step, 1)
                    dve.wait_ge(rec_step, n + 4 * c)

            def split_states(g):
                ts(z16[:, 0], z[:], 1.0, None, ALU.mult).then_inc(z_hi, 1)
                dve.wait_ge(z_hi, g + 1)
                tt(z16[:, 1], z[:], z16[:, 0], ALU.subtract).then_inc(z_lo, 1)
                dve.wait_ge(z_lo, g + 1)
                if known(g, 1):
                    dve.wait_ge(y_ready, BANKS * g)
                else:
                    dve.wait_ge(zeroed, 1)
                for j in range(J):
                    rows = slice(N * j, N * j + N)
                    ts(zdiag[rows, :, :, :, j].rearrange("p h q k c -> p (h q k) c"),
                       z16[rows].rearrange("p h q k c -> p (h q k) c"), 1.0, None, ALU.mult).then_inc(z_spread, 1)

            def lower_k(g):
                dve.wait_ge(k_hi, g + 1)
                tt(ksb[:, :, 1], psK[0:GC, 0:P], ksb[:, :, 0], ALU.subtract).then_inc(k_lo, 1)

            def body(g, p):
                if there(g):
                    recurrence(g, p, range(1, 3))
                if there(g + 1):
                    lower_im(g + 1, 1 - p)
                if there(g):
                    recurrence(g, p, range(3, C - 1))
                if there(g + 1):
                    lower_k(g + 1)
                if there(g + 2) and known(g, -1):
                    dve.wait_ge(im_lo, g + 2)
                    dve.wait_ge(carry_step, 3 * g + 6)
                    phases(dve, sh, g + 2)
                if there(g):
                    split_states(g)
                if there(g + 1):
                    scaled(g + 1)
                if there(g + 2):
                    tables(g + 2, p)
                if isinstance(g, int) and g == -2:
                    dve.memset(zdiag[:], 0.0).then_inc(zeroed, 1)
                if isinstance(g, int) and g == G:
                    for i in range(BANKS // 2, BANKS):
                        dve.wait_ge(hi_done, BANKS * (G - 1) + i + 1)
                        part = y16[:, (G - 1) * GC + i * BC:(G - 1) * GC + (i + 1) * BC]
                        tt(part[:, :, 1], gl[:, i], part[:, :, 0], ALU.subtract)

            ts(modes16[:, :, 0], sh["modes"][:, 2:4], 1.0, None, ALU.mult).then_inc(modes_hi, 1)
            dve.wait_ge(modes_hi, 1)
            tt(modes16[:, :, 1], sh["modes"][:, 2:4], modes16[:, :, 0], ALU.subtract).then_inc(modes_lo, 1)
            for k, sign in enumerate((1.0, -1.0)):
                ts(dd[:, :, k], sh["modes"][:, 4], sign, None, ALU.mult).then_inc(dd_ready, 1)
            dve.wait_ge(dd_ready, 2)
            rounds(dve, body)


def feed_forward(nc, io, sh):
    S = B * L // (ST * P)
    PAIRS = ST // 2
    LN_STEPS = 10
    TERMS = ((0, 0), (0, 1), (1, 0))
    with ExitStack() as ctx:
        def sb(name, shape, dt=F32):
            return ctx.enter_context(nc.sbuf_tensor(name, shape, dt))

        def psum(name, shape, dt=F32):
            return ctx.enter_context(nc.psum_tensor(name, shape, dt))

        def sem(name):
            return ctx.enter_context(nc.semaphore(name))

        w1_raw = sb("w1_raw", [P, KD, F])
        w2_raw = sb("w2_raw", [P, KF, D])
        w1 = sb("w1", [P, 2, 2, KD, F], F16)
        w2 = sb("w2", [P, 2, 2, KF, D], F16)
        b1_now = sb("b1_now", [P, 2, KF])
        b2 = sb("b2", [P, E, D])
        wp, bias, b1, id16, rev16 = (sh[k] for k in ("wp", "bias", "b1", "id16", "rev16"))
        xres = sb("xres", [P, 4, ST, D])
        yT = sb("yT", [P, 2, KD, 2, P], F16)
        z = sb("zproj", [P, ST, D])
        hin = sb("hin", [P, ST, D])
        hin16 = sb("hin16", [P, 2, ST, D], F16)
        hT = sb("hT", [P, 2, 2, KD, ST, P], F16)
        a32 = sb("a32", [P, 2, ST * P])
        a16 = sb("a16", [P, 2, KF, ST * P], F16)
        ff = sb("ff", [P, 2, ST, D])
        NA, NX, NB = range(3)
        stats = sb("stats_c", [P, 3, ST, 6])
        small = sb("small_c", [P, 3, 4, ST])
        var = sb("var", [P, 3, ST])
        rstd = sb("rstd_c", [P, 3, ST])
        nmr = sb("nmr", [P, 3, ST])
        minus_half = sb("minus_half_c", [P, ST])
        ps_yT = psum("ps_yT", [P, 2, KD, 2, P])
        ps_z = psum("ps_z", [P, 2, D])
        ps_hT = psum("ps_hT", [P, 2, KD, 2, P], F16)
        A_BANKS = 3
        ps_a = psum("ps_a", [P, A_BANKS, ST * P])
        ps_f1 = psum("ps_f1", [P, 2, D])
        ps_f = [ps_a[:, 2].rearrange("p (t d) -> p t d", t=2), ps_f1]

        b2_in, w1_in, w2_in, x_in, stored = (
            sem("b2_in"), sem("w1_in"), sem("w2_in"), [sem(f"x_in_c{k}") for k in range(4)],
            [sem("stored0"), sem("stored1")])
        cst, b1_ready, w1_hi, w1_lo, w2_hi, w2_lo = (
            sem("cst_c"), sem("b1_ready"), sem("w1_hi"), sem("w1_lo"), sem("w2_hi"), sem("w2_lo"))
        yT_ready, yT_done, z_ready, hT_ready, hT_done = (
            sem("yT_ready"), sem("yT_done"), sem("z_ready_c"), sem("hT_ready"), sem("hT_done"))
        a_ready, a_hi, a_lo, f_ready = sem("a_ready"), sem("a_hi"), sem("a_lo"), sem("f_ready")
        ln_step, ln_var, ln_rstd, ln_nmr, ln_done = (
            [sem(f"{n}{k}") for k in range(3)] for n in ("ln_step", "ln_var", "ln_rstd", "ln_nmr", "ln_done"))
        x1_done, hin_hi, hin_lo, out_ready = sem("x1_done"), sem("hin_hi"), sem("hin_lo"), sem("out_ready")
        z_half, x1_first, last_norm, last_out = sem("z_half"), sem("x1_first"), sem("last_norm"), sem("last_out")
        y16 = sh["xn"][:].bitcast(F16).rearrange("p d (k c) -> p d k c", k=2)

        def windows(body):
            def run(eng):
                body(0, 0)
                with eng.Fori(0, (S - 4) // 4) as i:
                    for k in range(4):
                        body(4 * i + k + 1, (k + 1) % 4)
                for s in range(S - 3, S):
                    body(s, s % 4)
            return run

        def known(s, least):
            return not isinstance(s, int) or s >= least

        def there(s):
            return not isinstance(s, int) or s < S

        def expert(s, k):
            if isinstance(s, int):
                return s // 2
            return (s - k) // 2 + k // 2

        block = ctx.enter_context(nc.Block())

        @block.sync
        def _(sp):
            def load_w1(e):
                sp.dma_start(w1_raw[:], io["w1"][bass.ds(e, 1)].rearrange("o (k p) f -> p (o k) f", p=P)).then_inc(w1_in, 16)

            def load_w2(e):
                sp.dma_start(w2_raw[:], io["w2"][bass.ds(e, 1)].rearrange("o (k p) d -> p (o k) d", p=P)).then_inc(w2_in, 16)

            def load_x(s, k):
                sp.dma_start(xres[:, k], io["x"].rearrange("b (u t p) d -> (b u) p t d", p=P, t=ST)[bass.ds(s, 1)]
                             .rearrange("o p t d -> p (o t) d")).then_inc(x_in[k], 16)

            def store(s, k):
                sp.wait_ge(out_ready, s + 1)
                sp.dma_start(io["out"].rearrange("b (u t p) d -> (b u) p t d", p=P, t=ST)[bass.ds(s, 1)]
                             .rearrange("o p t d -> p (o t) d"), ff[:, k % 2]).then_inc(stored[k % 2], 16)

            load_x(0, 0)
            load_w1(0)
            load_w2(0)
            for e in range(E):
                sp.dma_start(b2[:, e], io["b2"][e].partition_broadcast(P)).then_inc(b2_in, 16)
            load_x(1, 1)
            load_x(2, 2)
            sp.wait_ge(w1_lo, 1)
            load_w1(1)

            def body(s, k):
                if known(s, 1):
                    store(s - 1, k - 1)
                if there(s + 3):
                    load_x(s + 3, (k + 3) % 4)
                e = expert(s, k)
                if k % 2 == 0 and (not isinstance(s, int) or e + 1 < E):
                    sp.wait_ge(w2_lo, e + 1)
                    load_w2(e + 1)
                if k % 2 == 1 and (not isinstance(s, int) or e + 2 < E):
                    sp.wait_ge(w1_lo, e + 2)
                    load_w1(e + 2)

            windows(body)(sp)
            out = io["out"][B - 1, L - ST * P:L].rearrange("(t p) d -> p t d", p=P)
            for h in range(2):
                sp.wait_ge(last_out, h + 1)
                sp.dma_start(out[:, 2 * h:2 * h + 2], ff[:, 1, 2 * h:2 * h + 2]).then_inc(stored[1], 16)
            sp.wait_ge(stored[0], 16 * (S // 2))
            sp.wait_ge(stored[1], 16 * (S // 2) + 16)

        @block.gpsimd
        def _(pool):
            pool.memset(minus_half[:], -0.5).then_inc(cst, 1)
            pool.wait_ge(cst, 1)

            def power(n, s):
                pool.wait_ge(ln_var[n], s + 1)
                pool.tensor_tensor(rstd[:, n], var[:, n], minus_half[:], ALU.pow).then_inc(ln_rstd[n], 1)
                pool.wait_ge(ln_rstd[n], s + 1)
                pool.tensor_tensor(nmr[:, n], small[:, n, 0], rstd[:, n], ALU.mult).then_inc(ln_nmr[n], 1)

            def first_residual():
                for t in range(ST // 2):
                    last = pool.tensor_scalar(z[:, t], z[:, t], small[:, NA, 0, t:t + 1], rstd[:, NA, t:t + 1],
                                              ALU.add, ALU.mult)
                last.then_inc(ln_done[NA], 1)
                pool.wait_ge(x1_first, 1)
                pool.sem_inc(x1_done, 1)

            def residual(s, k):
                for t in range(ST):
                    last = pool.tensor_scalar(z[:, t], z[:, t], small[:, NA, 0, t:t + 1], rstd[:, NA, t:t + 1],
                                              ALU.add, ALU.mult)
                last.then_inc(ln_done[NA], 1)
                pool.wait_ge(ln_done[NA], s + 1)
                pool.wait_ge(x_in[k], 16 * (s // 4) + 16 if isinstance(s, int) else 4 * (s - k) + 16)
                pool.tensor_tensor(xres[:, k], xres[:, k], z[:], ALU.add).then_inc(x1_done, 1)

            def finish(s, k):
                pool.wait_ge(ln_done[NB], s + 1)
                pool.tensor_tensor(ff[:, k % 2], ff[:, k % 2], xres[:, k], ALU.add).then_inc(out_ready, 1)

            def body(s, k):
                if there(s + 1):
                    power(NA, s + 1)
                    residual(s + 1, (k + 1) % 4)
                if known(s, 1):
                    power(NB, s - 1)
                if there(s + 1):
                    power(NX, s + 1)
                if known(s, 1):
                    finish(s - 1, (k - 1) % 4)

            power(NA, 0)
            first_residual()
            power(NX, 0)
            windows(body)(pool)
            power(NB, S - 1)

        @block.scalar
        def _(act):
            def evacuate_yT(s, t):
                act.wait_ge(yT_ready, ST * s + t + 1)
                if known(s, 1) or t >= 2:
                    act.wait_ge(z_ready, PAIRS * s + t // 2)
                act.activation(yT[:, t % 2], ps_yT[:, t % 2], ACT.Copy).then_inc(yT_done, 1)

            def normalise(n, s, out, data):
                act.wait_ge(ln_nmr[n], s + 1)
                for t in range(ST):
                    last = act.activation(out[:, t], data[:, t], ACT.Identity, scale=rstd[:, n, t:t + 1],
                                          bias=nmr[:, n, t:t + 1])
                last.then_inc(ln_done[n], 1)

            def hidden(s, k, f):
                act.wait_ge(a_ready, KF * s + f + 1)
                if k % 2 == 0 and f == 0:
                    act.wait_ge(b1_ready, expert(s, k) + 1)
                b = b1_now[:, k // 2, f:f + 1]
                act.activation(a16[:, 0, f], ps_a[:, f % A_BANKS], ACT.Gelu_apprx_tanh, scale=1.0 / W_SCALE, bias=b)
                if known(s, 1) or f >= 2:
                    act.wait_ge(a_lo, KF * s + f - 1)
                act.activation(a32[:, f % 2], ps_a[:, f % A_BANKS], ACT.Gelu_apprx_tanh, scale=1.0 / W_SCALE,
                               bias=b).then_inc(a_hi, 1)

            def split_w1(e, ep):
                act.wait_ge(w1_in, 16 * e + 16)
                act.activation(w1[:, ep, 0], w1_raw[:], ACT.Copy, scale=W_SCALE).then_inc(w1_hi, 1)

            def split_w2(e, ep):
                act.wait_ge(w2_in, 16 * e + 16)
                act.activation(w2[:, ep, 0], w2_raw[:], ACT.Copy, scale=W_SCALE).then_inc(w2_hi, 1)

            def body(s, k):
                for f in range(KF):
                    hidden(s, k, f)
                if there(s + 2):
                    evacuate_yT(s + 2, 0)
                    evacuate_yT(s + 2, 1)
                if known(s, 1):
                    normalise(NB, s - 1, ff[:, (k - 1) % 2], ff[:, (k - 1) % 2])
                if there(s + 1):
                    normalise(NX, s + 1, hin, xres[:, (k + 1) % 4])
                if there(s + 2):
                    evacuate_yT(s + 2, 2)
                    evacuate_yT(s + 2, 3)
                e = expert(s, k)
                if k % 2 == 0 and (not isinstance(s, int) or e + 1 < E):
                    split_w1(e + 1, (k // 2 + 1) % 2)
                if k % 2 == 1 and (not isinstance(s, int) or e + 1 < E):
                    split_w2(e + 1, (k // 2 + 1) % 2)

            for t in range(ST):
                evacuate_yT(0, t)
            split_w1(0, 0)
            split_w2(0, 0)
            act.wait_ge(ln_nmr[NA], 1)
            for t in range(ST // 2, ST):
                last = act.activation(z[:, t], z[:, t], ACT.Identity, scale=rstd[:, NA, t:t + 1],
                                      bias=nmr[:, NA, t:t + 1])
            last.then_inc(z_half, 1)
            for t in range(ST):
                evacuate_yT(1, t)
            normalise(NX, 0, hin, xres[:, 0])
            windows(body)(act)
            act.wait_ge(ln_nmr[NB], S)
            for t in range(ST):
                last = act.activation(ff[:, 1, t], ff[:, 1, t], ACT.Identity, scale=rstd[:, NB, t:t + 1],
                                      bias=nmr[:, NB, t:t + 1])
                if t % 2 == 1:
                    last.then_inc(last_norm, 1)

        @block.tensor
        def _(pe):
            def turn_y(s, k, t):
                if known(s, 1) or t >= 2:
                    pe.wait_ge(yT_done, ST * s + t - 1)
                e = expert(s, k)
                c = (k % 2) * ST + t
                for h in range(KD):
                    for part in range(2):
                        tile = y16[:, h * P:(h + 1) * P, part, bass.ds(c * B + e, 1)].rearrange("p d o -> p (d o)")
                        last = pe.matmul(ps_yT[:, t % 2, h, part], tile, rev16[:], start=True, stop=True)
                last.then_inc(yT_ready, 1)

            def project(s, r):
                if known(s, 1) or r == 1:
                    pe.wait_ge(ln_step[NA], LN_STEPS * s + 1 if r == 1 else LN_STEPS * s - LN_STEPS + 3)
                for t in range(2):
                    pe.wait_ge(yT_done, ST * s + 2 * r + t + 1)
                    n = 0
                    for wk, yk in TERMS:
                        for h in range(KD):
                            last = pe.matmul(ps_z[:, t], yT[:, t, h, yk], wp[:, wk, h], start=(n == 0), stop=(n == 5))
                            n += 1
                last.then_inc(z_ready, 1)

            def turn_h(s, r):
                pe.wait_ge(hin_lo, s + 1)
                if known(s, 1) or r == 1:
                    pe.wait_ge(hT_done, PAIRS * s + r)
                for t in range(2):
                    for h in range(KD):
                        for part in range(2):
                            last = pe.transpose(ps_hT[:, t, h, part], hin16[:, part, 2 * r + t, h * P:(h + 1) * P], id16[:])
                last.then_inc(hT_ready, 1)

            def layer1(s, k, f):
                ep = k // 2
                if f >= A_BANKS:
                    pe.wait_ge(a_hi, KF * s + f - A_BANKS + 1)
                elif known(s, 1):
                    pe.wait_ge(a_hi, KF * s)
                    if f == 2:
                        pe.wait_ge(ln_step[NB], LN_STEPS * s - LN_STEPS + 1)
                n = 0
                for wk, xk in TERMS:
                    for h in range(KD):
                        last = pe.matmul(ps_a[:, f % A_BANKS], w1[:, ep, wk, h, f * P:(f + 1) * P],
                                         hT[:, k % 2, xk, h].rearrange("p t n -> p (t n)"), start=(n == 0), stop=(n == 5))
                        n += 1
                last.then_inc(a_ready, 1)

            def layer2(s, k, t):
                ep = k // 2
                if t == 0:
                    pe.wait_ge(a_hi, KF * s + 6)
                if t == 2 and known(s, 1):
                    pe.wait_ge(ln_step[NB], LN_STEPS * s - LN_STEPS + 3)
                for f in range(KF):
                    if t == 0:
                        pe.wait_ge(a_lo, KF * s + f + 1)
                    for n, (wk, ak) in enumerate(TERMS):
                        last = pe.matmul(ps_f[t // 2][:, t % 2], a16[:, ak, f, t * P:(t + 1) * P], w2[:, ep, wk, f],
                                         start=(f == 0 and n == 0), stop=(f == KF - 1 and n == 2))
                if t % 2 == 1:
                    last.then_inc(f_ready, 1)

            def body(s, k):
                pe.wait_ge(hT_done, PAIRS * s + PAIRS)
                if k % 2 == 0:
                    pe.wait_ge(w1_lo, expert(s, k) + 1)
                for f in range(KF):
                    layer1(s, k, f)
                nxt, nk, far, fk = s + 1, (k + 1) % 4, s + 2, (k + 2) % 4
                if there(far):
                    turn_y(far, fk, 0)
                    turn_y(far, fk, 1)
                if k % 2 == 0:
                    pe.wait_ge(w2_lo, expert(s, k) + 1)
                layer2(s, k, 0)
                layer2(s, k, 1)
                if there(far):
                    project(far, 0)
                    turn_y(far, fk, 2)
                    turn_y(far, fk, 3)
                layer2(s, k, 2)
                if there(nxt):
                    turn_h(nxt, 0)
                layer2(s, k, 3)
                if there(nxt):
                    turn_h(nxt, 1)
                if there(far):
                    project(far, 1)

            turn_y(0, 0, 0)
            turn_y(0, 0, 1)
            project(0, 0)
            turn_y(0, 0, 2)
            turn_y(0, 0, 3)
            project(0, 1)
            turn_y(1, 1, 0)
            turn_y(1, 1, 1)
            project(1, 0)
            turn_y(1, 1, 2)
            turn_y(1, 1, 3)
            project(1, 1)
            turn_h(0, 0)
            turn_h(0, 1)
            windows(body)(pe)

        @block.vector
        def _(dve):
            tt, ts, stt = dve.tensor_tensor, dve.tensor_scalar, dve.scalar_tensor_tensor

            def biased(n, s, r, out, data, scale, b):
                stt(out=out[:, 2 * r:2 * r + 2], in0=data, scalar=scale, in1=b.unsqueeze(1).broadcast_to([P, 2, D]),
                    op0=ALU.mult, op1=ALU.add).then_inc(ln_step[n], 1)
                dve.wait_ge(ln_step[n], LN_STEPS * s + 2 * r + 1)
                for t in range(2 * r, 2 * r + 2):
                    last = dve.bn_stats(stats[:, n, t], out[:, t])
                last.then_inc(ln_step[n], 1)

            def variance(n, s):
                st = [stats[:, n, :, k] for k in range(6)]
                sm = [small[:, n, k] for k in range(4)]
                if known(s, 1):
                    dve.wait_ge(ln_nmr[n], s)
                dve.wait_ge(ln_step[n], LN_STEPS * s + 4)
                tt(sm[0], st[1], st[4], ALU.add).then_inc(ln_step[n], 1)
                tt(sm[1], st[1], st[4], ALU.subtract).then_inc(ln_step[n], 1)
                tt(sm[2], st[2], st[5], ALU.add).then_inc(ln_step[n], 1)
                dve.wait_ge(ln_step[n], LN_STEPS * s + 7)
                stt(out=sm[3], in0=sm[1], scalar=0.25, in1=sm[1], op0=ALU.mult, op1=ALU.mult).then_inc(ln_step[n], 1)
                ts(sm[2], sm[2], 1.0 / D, EPS, ALU.mult, ALU.add).then_inc(ln_step[n], 1)
                ts(sm[0], sm[0], -0.5, None, ALU.mult).then_inc(ln_step[n], 1)
                dve.wait_ge(ln_step[n], LN_STEPS * s + 10)
                tt(var[:, n], sm[2], sm[3], ALU.add).then_inc(ln_var[n], 1)

            def z_pair(s, r):
                dve.wait_ge(z_ready, PAIRS * s + r + 1)
                if r == 0 and known(s, 1):
                    dve.wait_ge(x1_done, s)
                biased(NA, s, r, z, ps_z[:], 1.0 / W_SCALE, bias[:])

            def f_pair(s, k, r):
                dve.wait_ge(f_ready, PAIRS * s + r + 1)
                if r == 0 and known(s, 2):
                    dve.wait_ge(stored[k % 2], stored_count(s, k))
                if isinstance(s, int) and s == 0 and r == 0:
                    dve.wait_ge(b2_in, 16 * E)
                e = expert(s, k)
                biased(NB, s, r, ff[:, k % 2], ps_f[r][:], 1.0 / W_SCALE, b2[:, bass.ds(e, 1)].rearrange("p o d -> p (o d)"))

            def stored_count(s, k):
                return 16 * (s // 2) if isinstance(s, int) else 8 * (s - k % 2)

            def x1_statistics(s, k):
                if isinstance(s, int) and s == 0:
                    dve.wait_ge(ln_done[NA], 1)
                    dve.wait_ge(z_half, 1)
                    dve.wait_ge(x_in[0], 16)
                    tt(xres[:, k], xres[:, k], z[:], ALU.add).then_inc(x1_first, 1)
                    dve.wait_ge(x1_first, 1)
                else:
                    dve.wait_ge(x1_done, s + 1)
                for t in range(ST):
                    last = dve.bn_stats(stats[:, NX, t], xres[:, k, t])
                last.then_inc(ln_step[NX], 4)
                variance(NX, s)

            def split_h(s):
                dve.wait_ge(ln_done[NX], s + 1)
                if known(s, 1):
                    dve.wait_ge(hT_ready, PAIRS * s)
                ts(hin16[:, 0], hin[:], 1.0, None, ALU.mult).then_inc(hin_hi, 1)
                dve.wait_ge(hin_hi, s + 1)
                tt(hin16[:, 1], hin[:], hin16[:, 0], ALU.subtract).then_inc(hin_lo, 1)

            def evacuate_h(s, k, r):
                dve.wait_ge(hT_ready, PAIRS * s + r + 1)
                for h in range(KD):
                    last = dve.tensor_copy(
                        hT[:, k % 2, :, h, 2 * r:2 * r + 2], ps_hT[:, :, h].rearrange("p t k n -> p k t n"))
                last.then_inc(hT_done, 1)

            def lower(s, f):
                dve.wait_ge(a_hi, KF * s + f + 1)
                tt(a16[:, 1, f], a32[:, f % 2], a16[:, 0, f], ALU.subtract).then_inc(a_lo, 1)

            def split_w(e, ep, w, raw, hi, lo):
                dve.wait_ge(hi, e + 1)
                stt(out=w[:, ep, 1], in0=raw[:], scalar=W_SCALE, in1=w[:, ep, 0], op0=ALU.mult,
                    op1=ALU.subtract).then_inc(lo, 1)

            def next_b1(e, ep):
                ts(b1_now[:, ep], b1[:, bass.ds(e * KF, KF)], 1.0, None, ALU.mult).then_inc(b1_ready, 1)

            def body(s, k):
                nxt, nk, far, fk = s + 1, (k + 1) % 4, s + 2, (k + 2) % 4
                lower(s, 0)
                if there(nxt):
                    z_pair(nxt, 1)
                lower(s, 1)
                if there(nxt):
                    variance(NA, nxt)
                lower(s, 2)
                if known(s, 1):
                    f_pair(s - 1, (k - 1) % 4, 1)
                lower(s, 3)
                if known(s, 1):
                    variance(NB, s - 1)
                for f in range(4, KF):
                    lower(s, f)
                if there(nxt):
                    x1_statistics(nxt, nk)
                if there(nxt):
                    split_h(nxt)
                if there(far):
                    z_pair(far, 0)
                f_pair(s, k, 0)
                if there(nxt):
                    evacuate_h(nxt, nk, 0)
                    evacuate_h(nxt, nk, 1)
                e = expert(s, k)
                if k % 2 == 0 and (not isinstance(s, int) or e + 1 < E):
                    split_w(e + 1, (k // 2 + 1) % 2, w1, w1_raw, w1_hi, w1_lo)
                if k % 2 == 1 and (not isinstance(s, int) or e + 1 < E):
                    split_w(e + 1, (k // 2 + 1) % 2, w2, w2_raw, w2_hi, w2_lo)
                    next_b1(e + 1, (k // 2 + 1) % 2)

            z_pair(0, 0)
            z_pair(0, 1)
            variance(NA, 0)
            next_b1(0, 0)
            split_w(0, 0, w1, w1_raw, w1_hi, w1_lo)
            x1_statistics(0, 0)
            z_pair(1, 0)
            split_w(0, 0, w2, w2_raw, w2_hi, w2_lo)
            split_h(0)
            evacuate_h(0, 0, 0)
            evacuate_h(0, 0, 1)
            windows(body)(dve)
            f_pair(S - 1, (S - 1) % 4, 1)
            variance(NB, S - 1)
            for h in range(2):
                dve.wait_ge(last_norm, h + 1)
                half = slice(2 * h, 2 * h + 2)
                tt(ff[:, 1, half], ff[:, 1, half], xres[:, 3, half], ALU.add).then_inc(last_out, 1)


def sandwich(nc, io):
    with ExitStack() as ctx:
        sh = {"const": ctx.enter_context(nc.sbuf_tensor("constants", [P, C_END], F32)),
              "wp": ctx.enter_context(nc.sbuf_tensor("wp", [P, 2, KD, D], F16)),
              "bias": ctx.enter_context(nc.sbuf_tensor("bias", [P, D], F32)),
              "b1": ctx.enter_context(nc.sbuf_tensor("b1", [P, E * KF], F32)),
              "id16": ctx.enter_context(nc.sbuf_tensor("id16", [P, P], F16)),
              "rev16": ctx.enter_context(nc.sbuf_tensor("rev16", [P, P], F16)),
              "xn": ctx.enter_context(nc.sbuf_tensor("xn", [P, D, CB], F32))}
        with ExitStack() as mixer:
            sh["mag"] = mixer.enter_context(nc.sbuf_tensor("magnitudes", [P, Q, T], F32))
            for name in ("turns", "im", "re"):
                sh[name] = mixer.enter_context(nc.sbuf_tensor(name, [P, GQ, T], F32))
            for name in ("turns_done", "frac_step", "trig_step"):
                sh[name] = mixer.enter_context(nc.semaphore(name))
            sh["half_pi"] = mixer.enter_context(nc.sbuf_tensor("half_pi", [P, 1], F32))
            sh["modes"] = mixer.enter_context(nc.sbuf_tensor("modes", [P, 6, Q], F32))
            mixer_prologue(nc, io, sh)
            mixer_groups(nc, io, sh)
        feed_forward(nc, io, sh)


_INS = ["L0_attn_x", "L0_attn_log_dt", "L0_attn_log_A_real", "L0_attn_A_imag", "L0_attn_C_real", "L0_attn_C_imag",
        "L0_attn_W", "L0_attn_b", "L0_ffn_w1", "L0_ffn_b1", "L0_ffn_w2", "L0_ffn_b2"]


def kernel(**inputs):
    import numpy as _np
    import concourse.bacc as _bacc
    from concourse import mybir as _mybir
    from concourse.bass_utils import run_bass_kernel_spmd as _run

    nc = _bacc.Bacc("TRN2", target_bir_lowering=False, num_devices=1)
    arrays, io = {}, {}
    for name in _INS:
        a = _np.ascontiguousarray(inputs[name])
        arrays[f"in_{name}_dram"] = a
        io[name.split("_", 2)[2]] = nc.dram_tensor(
            f"in_{name}_dram", a.shape, _mybir.dt.from_np(a.dtype), kind="ExternalInput").ap()
    const = _np.zeros((P, C_END), _np.float32)
    const[:, C_ID:C_ID + P] = _np.eye(P)
    const[:, C_REV:C_REV + P] = _np.eye(P)[::-1]
    const[:, C_POW:C_POW + P] = _np.arange(P)[::-1]
    const[:, C_POW + P] = P
    mask = const[:, C_MASK:].reshape(P, GQ, GC)
    for q in range(GQ):
        for j in range(J):
            mask[j * N:(j + 1) * N, q, J * q + j] = 1.0
    arrays["in_const_dram"] = const
    io["const"] = nc.dram_tensor("in_const_dram", const.shape, _mybir.dt.float32, kind="ExternalInput").ap()
    io["kpad"] = nc.dram_tensor("kpad", [D, 2 * P, 2], _mybir.dt.float16, kind="Internal").ap()
    io["out"] = nc.dram_tensor("out_0_dram", [B, L, D], _mybir.dt.float32, kind="ExternalOutput").ap()
    sandwich(nc, io)
    r = _run(nc, [arrays], core_ids=[0])
    return r.results[0]["out_0_dram"]
```
